# Optimizing a Trainium2 kernel written in Bass

```python
import numpy as np
import jax
import jax.numpy as jnp

def _softmax(x, axis=-1):
    return jax.nn.softmax(x, axis=axis)

def _gelu(x):
    return jax.nn.gelu(x, approximate=True)

def _silu(x):
    return jax.nn.silu(x)

def _sigmoid(x):
    return jax.nn.sigmoid(x)

def _layernorm(x, axis=-1, eps=1e-05):
    m = jnp.mean(x, axis=axis, keepdims=True)
    v = jnp.var(x, axis=axis, keepdims=True)
    return (x - m) / jnp.sqrt(v + eps)

def _scatter_add(tgt, idx, src, axis=0):
    return tgt.at[idx].add(src)

def _segment_sum(src, seg, n):
    return jax.ops.segment_sum(src, seg, n)
kernel_name = 'mk_flamingo_gated_d1_seqx_r8_b4b61e'

def setup_inputs(seed: int=0):
    np.random.seed(seed)
    _w = jnp.asarray

    def _rec_inputs():
        import jax
        import jax.numpy as jnp
        _rk = jax.random.key(seed)
        x = 2.818e-05 + 1 * jax.random.normal(jax.random.fold_in(_rk, 1), (16, 128, 128), jnp.float32)
        _lenS = 128 - jax.random.randint(jax.random.fold_in(_rk, 7), (16,), 0, max(1, 128 // 4) + 1, jnp.int32)
        _lenS2 = 128 - jax.random.randint(jax.random.fold_in(_rk, 8), (16,), 0, max(1, 128 // 4) + 1, jnp.int32)
        _ctx_2048P = jax.random.normal(jax.random.fold_in(_rk, 11), (16, 16, 256), jnp.float32)
        _ctx_2048c = jax.random.dirichlet(jax.random.fold_in(_rk, 511), 0.3 * jnp.ones((16,), jnp.float32), (16, 128))
        _ctx_2048t = jnp.einsum('bsk,bkd->bsd', _ctx_2048c, _ctx_2048P)
        _ctx_2048t = _ctx_2048t * jax.lax.rsqrt(jnp.mean(jnp.square(_ctx_2048t)) + 1e-12) * 0.953939
        ctx_2048 = -0.000125008 + 0.999885 * (_ctx_2048t + 0.3 * jax.random.normal(jax.random.fold_in(_rk, 611), (16, 128, 256), jnp.float32))
        _validS = jnp.arange(128)[None, :] < _lenS[:, None]
        _validS2 = jnp.arange(128)[None, :] < _lenS2[:, None]
        _causal = jnp.tril(jnp.ones((128, 128), dtype=bool))
        mask_BxS2_fk1 = jnp.where(jnp.broadcast_to(_validS2[:, :], (16, 128)), 1.0, 0.0).astype(jnp.float32)
        _g = jax.random.normal(jax.random.fold_in(_rk, 9001), (2, 1), jnp.float32)
        _g = jnp.sign(_g) * jnp.maximum(jnp.abs(_g), 1.0) + (_g == 0) * 1.0
        g_xattn = _g[0]
        g_ffn = _g[1]
        return (x, ctx_2048, mask_BxS2_fk1, g_xattn, g_ffn)
    x, ctx_2048, mask_BxS2_fk1, g_xattn, g_ffn = _rec_inputs()

    def _L0_xattn_setup():
        import jax, jax.numpy as jnp
        import numpy as np
        B, S, T = (32, 64, 64)
        SRC_SIZE, TGT_SIZE, OUT_SIZE, NUM_HEAD = (256, 128, 128, 8)
        HEAD_DIM = OUT_SIZE // NUM_HEAD
        key = jax.random.key(seed)
        ks = jax.random.split(key, 12)
        src = jax.random.normal(ks[0], (B, S, SRC_SIZE), dtype=jnp.float32)
        tgt = jax.random.normal(ks[1], (B, T, TGT_SIZE), dtype=jnp.float32)
        src_mask = (jax.random.uniform(ks[2], (B, S)) > 0.3).astype(jnp.float32)
        src_mask = src_mask.at[:, 0].set(1.0)
        tgt_mask = (jax.random.uniform(ks[3], (B, T)) > 0.3).astype(jnp.float32)
        tgt_mask = tgt_mask.at[:, 0].set(1.0)

        def lin(k, out_f, in_f):
            return jax.random.normal(k, (out_f, in_f), dtype=jnp.float32) / np.sqrt(in_f)
        W_src = lin(ks[4], 2 * OUT_SIZE, SRC_SIZE)
        b_src = jnp.zeros((2 * OUT_SIZE,), jnp.float32)
        W_tgt = lin(ks[5], OUT_SIZE, TGT_SIZE)
        b_tgt = jnp.zeros((OUT_SIZE,), jnp.float32)
        W_out = lin(ks[6], OUT_SIZE, OUT_SIZE + TGT_SIZE)
        b_out = jnp.zeros((OUT_SIZE,), jnp.float32)
        return {'src': src, 'tgt': tgt, 'src_mask': src_mask, 'tgt_mask': tgt_mask, 'W_src': W_src, 'b_src': b_src, 'W_tgt': W_tgt, 'b_tgt': b_tgt, 'W_out': W_out, 'b_out': b_out}
    _L0_xattn_all = _L0_xattn_setup()
    _L0_xattn_in = {k: v for k, v in _L0_xattn_all.items() if k in ('W_src', 'b_src', 'W_tgt', 'b_tgt', 'W_out', 'b_out')}
    del _L0_xattn_all

    def _L0_ffn_setup():
        import jax, jax.numpy as jnp
        import numpy as np
        TOP_K = 2
        ROUTE_SCALE = 1.0
        EPS = 1e-20
        key = jax.random.key(seed)
        ks = jax.random.split(key, 8)
        dim, hid, E, X = (128, 352, 8, 1)
        std = 0.02
        x = jax.random.normal(ks[0], (2, 256, dim), dtype=jnp.float32)
        w1 = jax.random.normal(ks[1], (E, hid, dim), dtype=jnp.float32) * std
        w2 = jax.random.normal(ks[2], (E, dim, hid), dtype=jnp.float32) * std
        w3 = jax.random.normal(ks[3], (E, hid, dim), dtype=jnp.float32) * std
        new_w1 = jax.random.normal(ks[4], (X, hid, dim), dtype=jnp.float32) * std
        new_w2 = jnp.zeros((X, dim, hid), dtype=jnp.float32)
        new_w3 = jax.random.normal(ks[5], (X, hid, dim), dtype=jnp.float32) * std
        gate_weight = jax.random.normal(ks[6], (E, dim), dtype=jnp.float32) * std
        new_gate_weight = jax.random.normal(ks[7], (X, dim), dtype=jnp.float32) * std
        gate_bias = jnp.zeros((X,), dtype=jnp.float32)
        return dict(x=x, w1=w1, w2=w2, w3=w3, new_w1=new_w1, new_w2=new_w2, new_w3=new_w3, gate_weight=gate_weight, new_gate_weight=new_gate_weight, gate_bias=gate_bias)
    _L0_ffn_all = _L0_ffn_setup()
    _L0_ffn_in = {k: v for k, v in _L0_ffn_all.items() if k in ('w1', 'w2', 'w3', 'new_w1', 'new_w2', 'new_w3', 'gate_weight', 'new_gate_weight', 'gate_bias')}
    del _L0_ffn_all
    return {'x': x, 'ctx_2048': ctx_2048, 'mask_BxS2_fk1': mask_BxS2_fk1, 'g_xattn': g_xattn, 'g_ffn': g_ffn, 'L0_xattn_W_src': _L0_xattn_in['W_src'], 'L0_xattn_b_src': _L0_xattn_in['b_src'], 'L0_xattn_W_tgt': _L0_xattn_in['W_tgt'], 'L0_xattn_b_tgt': _L0_xattn_in['b_tgt'], 'L0_xattn_W_out': _L0_xattn_in['W_out'], 'L0_xattn_b_out': _L0_xattn_in['b_out'], 'L0_ffn_w1': _L0_ffn_in['w1'], 'L0_ffn_w2': _L0_ffn_in['w2'], 'L0_ffn_w3': _L0_ffn_in['w3'], 'L0_ffn_new_w1': _L0_ffn_in['new_w1'], 'L0_ffn_new_w2': _L0_ffn_in['new_w2'], 'L0_ffn_new_w3': _L0_ffn_in['new_w3'], 'L0_ffn_gate_weight': _L0_ffn_in['gate_weight'], 'L0_ffn_new_gate_weight': _L0_ffn_in['new_gate_weight'], 'L0_ffn_gate_bias': _L0_ffn_in['gate_bias']}

def reference(x, ctx_2048, mask_BxS2_fk1, g_xattn, g_ffn, L0_xattn_W_src, L0_xattn_b_src, L0_xattn_W_tgt, L0_xattn_b_tgt, L0_xattn_W_out, L0_xattn_b_out, L0_ffn_w1, L0_ffn_w2, L0_ffn_w3, L0_ffn_new_w1, L0_ffn_new_w2, L0_ffn_new_w3, L0_ffn_gate_weight, L0_ffn_new_gate_weight, L0_ffn_gate_bias):
    import jax
    import jax.numpy as jnp

    def _L0_xattn_ref(src, tgt, src_mask, tgt_mask, W_src, b_src, W_tgt, b_tgt, W_out, b_out):
        import jax, jax.numpy as jnp
        import numpy as np
        B, S, T = (32, 64, 64)
        SRC_SIZE, TGT_SIZE, OUT_SIZE, NUM_HEAD = (256, 128, 128, 8)
        HEAD_DIM = OUT_SIZE // NUM_HEAD
        b, s, _ = src.shape
        t = tgt.shape[1]
        src_trans = jnp.einsum('bsf,of->bso', src, W_src) + b_src
        tgt_trans = jnp.einsum('btf,of->bto', tgt, W_tgt) + b_tgt
        src_trans = src_trans * src_mask[:, :, None]
        tgt_trans = tgt_trans * tgt_mask[:, :, None]
        src_key, src_val = jnp.split(src_trans, 2, axis=2)
        k = src_key.reshape(b, s, NUM_HEAD, HEAD_DIM)
        v = src_val.reshape(b, s, NUM_HEAD, HEAD_DIM)
        q = tgt_trans.reshape(b, t, NUM_HEAD, HEAD_DIM)
        scores = jnp.einsum('bthd,bshd->bhts', q, k) / np.sqrt(HEAD_DIM)
        scores = jnp.where(src_mask[:, None, None, :] == 0, -jnp.inf, scores)
        attn = jax.nn.softmax(scores, axis=-1)
        tgt_update = jnp.einsum('bhts,bshd->bthd', attn, v).reshape(b, t, OUT_SIZE)
        cat_tgt = jnp.concatenate([tgt, tgt_update], axis=2)
        return jnp.einsum('btf,of->bto', cat_tgt, W_out) + b_out

    def _L0_ffn_ref(x, w1, w2, w3, new_w1, new_w2, new_w3, gate_weight, new_gate_weight, gate_bias):
        import jax, jax.numpy as jnp
        import numpy as np
        TOP_K = 2
        ROUTE_SCALE = 1.0
        EPS = 1e-20
        bs, slen, dim = x.shape
        x_flat = x.reshape(-1, dim)
        ew1 = jnp.concatenate([w1, new_w1], axis=0)
        ew2 = jnp.concatenate([w2, new_w2], axis=0)
        ew3 = jnp.concatenate([w3, new_w3], axis=0)
        gate = jnp.concatenate([gate_weight, new_gate_weight], axis=0)
        e_orig = w1.shape[0]
        e_tot = gate.shape[0]
        bias = jnp.concatenate([jnp.zeros((e_orig,), x.dtype), gate_bias])
        scores = jax.nn.sigmoid((x_flat @ gate.T + bias).astype(jnp.float32))
        top_scores, selected = jax.lax.top_k(scores, TOP_K)
        top_scores = top_scores / (jnp.sum(top_scores, axis=-1, keepdims=True) + EPS)
        top_scores = top_scores * ROUTE_SCALE
        onehot = jax.nn.one_hot(selected, e_tot, dtype=jnp.float32)
        cw = jnp.einsum('tk,tke->te', top_scores, onehot)
        out = jnp.zeros_like(x_flat)
        for e in range(e_tot):
            h = jax.nn.silu(x_flat @ ew1[e].T) * (x_flat @ ew3[e].T)
            out = out + cw[:, e:e + 1] * (h @ ew2[e].T)
        return out.reshape(bs, slen, dim)
    x = x + jnp.tanh(g_xattn[0]) * _L0_xattn_ref(ctx_2048, _layernorm(x, axis=-1), mask_BxS2_fk1, mask_BxS2_fk1, L0_xattn_W_src, L0_xattn_b_src, L0_xattn_W_tgt, L0_xattn_b_tgt, L0_xattn_W_out, L0_xattn_b_out)
    x = x + jnp.tanh(g_ffn[0]) * _L0_ffn_ref(_layernorm(x, axis=-1), L0_ffn_w1, L0_ffn_w2, L0_ffn_w3, L0_ffn_new_w1, L0_ffn_new_w2, L0_ffn_new_w3, L0_ffn_gate_weight, L0_ffn_new_gate_weight, L0_ffn_gate_bias)
    return x

_drawn_inputs = setup_inputs


def setup_inputs(seed=0):
    import zlib

    import numpy as np

    out = dict(_drawn_inputs(seed))
    spreads = {'L0_xattn_b_src': (0.0, 0.1),
     'L0_xattn_b_tgt': (0.0, 0.8),
     'L0_xattn_b_out': (0.0, 0.1),
     'L0_ffn_new_w2': (0.0, 0.8)}
    factors = {'L0_ffn_w1': 8.0,
     'L0_ffn_w2': 8.0,
     'L0_ffn_w3': 8.0,
     'L0_ffn_new_w1': 5.917,
     'L0_ffn_new_w3': 5.871,
     'L0_ffn_gate_weight': 7.78,
     'L0_ffn_new_gate_weight': 6.76}
    for name, (base, spread) in spreads.items():
        noise = np.random.default_rng([zlib.crc32(name.encode()), seed]).standard_normal(out[name].shape)
        drawn = base * np.exp(spread * noise) if base else spread * noise
        out[name] = jnp.asarray(drawn.astype(out[name].dtype))
    for name, factor in factors.items():
        out[name] = (out[name] * factor).astype(out[name].dtype)
    return out
```

```python
from contextlib import ExitStack

import concourse.bass as bass
from concourse import mybir

ALU = mybir.AluOpType
ACT = mybir.ActivationFunctionType
AX = mybir.AxisListType
F32 = mybir.dt.float32
BF16 = mybir.dt.bfloat16

P = 128
NB = 16
D = 128
FC = 2
H, HD = 8, 16
HP = 32
UN = 4
NG = NB // UN
GT = UN * P
NE, HID = 9, 352
CH = [(0, 128), (128, 128), (256, 96)]
NC = len(CH)
KH_POOL, KH_DVE = 2, 5
WR = 3
SCALE = HD ** -0.5
MASKED = -1.0e30
LN_EPS = 1e-5
TOP_EPS = 1e-20
KNEE = 8.0
FLOOR = -88.72
STRETCH = 1024.0
TAKEN = -1.0e6
NCONST = P + H + NE


def build(nc, x, ctxT, mask, maskT, g2, consts, w_srcT, b_src, w_tgtT, b_tgt, w_outT, b_out,
          w13T, w2T, gateT, gate_b, out):
    with ExitStack() as ctx:
        def sb(name, shape, dt=F32):
            return ctx.enter_context(nc.sbuf_tensor(name, shape, dt))

        def ps(name, shape):
            return ctx.enter_context(nc.psum_tensor(name, shape, F32))

        def sem(name):
            return ctx.enter_context(nc.semaphore(name))

        cst = sb("cst", [P, NCONST])
        ident, head_rows, low_first = cst[:, 0:P], cst[:, P:P + H], cst[:, P + H:NCONST]
        gates, tgates = sb("gates", [P, 2]), sb("tgates", [P, 2])
        w_src = sb("w_src", [P, FC, 2 * D])
        w_tgt = sb("w_tgt", [P, D])
        w_out, w_outg = sb("w_out", [P, 2, D]), sb("w_outg", [P, 2, D])
        b_key, b_qry = sb("b_key", [P, 1]), sb("b_qry", [P, 1])
        b_val = sb("b_val", [P, D])
        b_res, b_resg = sb("b_res", [P, D]), sb("b_resg", [P, D])
        mask_t, live_t = sb("mask_t", [P, NB]), sb("live_t", [P, NB])
        mask_b = sb("mask_b", [P, NB * P])
        bias_b = sb("bias_b", [P, NB * P], BF16)
        share = sb("share", [P, P], BF16)
        minus_half = sb("minus_half", [P, UN])

        xs = sb("xs", [P, NB, D])
        st1, mv1 = sb("st1", [P, NB, 6]), sb("mv1", [P, NB, 2])
        ve1, rs1 = sb("ve1", [P, NB]), sb("rs1", [P, NB])
        xn1, xn1T = sb("xn1", [P, 2, UN, D]), sb("xn1T", [P, 2, GT])
        ctx_r = sb("ctx_r", [P, 2, FC, GT])
        kT = sb("kT", [P, 2, GT])
        qT = sb("qT", [P, NB * P])
        kheads = sb("kheads", [P, H, NB * P])
        vals = sb("vals", [P, NB, D])

        q_cur = sb("q_cur", [P, UN, P])
        v_cur = sb("v_cur", [P, UN, H, HP])
        mx = sb("mx", [P, 2, H])
        shifted, probs = sb("shifted", [P, 2, H, P]), sb("probs", [P, 2, H, P])
        probsT = sb("probsT", [P, 2, H, P])
        oT = sb("oT", [P, 2, 2, P])
        rden, upd, updT = sb("rden", [P, 2, H]), sb("upd", [P, 2, D]), sb("updT", [P, 2, P])
        st2, mv2, ve2, rs2 = sb("st2", [P, 2, 6]), sb("mv2", [P, 2, 2]), sb("ve2", [P, 2]), sb("rs2", [P, 2])
        x2, xn2 = sb("x2", [P, 2, D]), sb("xn2", [P, 2, D])
        xn2T = sb("xn2T", [P, NB * P])

        gate_w, gate_bb = sb("gate_w", [P, NE]), sb("gate_bb", [P, NE])
        lgT = sb("lgT", [NE, NB * P])
        z, sig, key, pick = (sb(n, [P, NB, NE]) for n in ("z", "sig", "key", "pick"))
        one, two, cw = (sb(n, [P, NB, NE]) for n in ("one", "two", "cw"))
        high = sb("high", [P, NB * NE + 1])
        best, first, total = (sb(n, [P, NB]) for n in ("best", "first", "total"))
        w13 = sb("w13", [P, WR, 2, HID])
        w2 = sb("w2", [P, WR, NC, D])
        gated = shifted[:].rearrange("p a h t -> p (a h t)")[:, 0:NC * GT].rearrange("p (c t) -> p c t", c=NC)
        hidT = probs[:].rearrange("p a h t -> p (a h t)")[:, 0:NC * GT].rearrange("p (c t) -> p c t", c=NC)

        score_ps = ps("score_ps", [P, 2, H, P])
        pt_ps = ps("pt_ps", [P, 2, UN, P])
        ps_a, ps_b = ps("ps_a", [P, GT]), ps("ps_b", [P, GT])
        bank = [score_ps[:, i // 2, UN * (i % 2):UN * (i % 2) + UN, :] for i in range(4)]
        bank += [pt_ps[:, 0, :, :], pt_ps[:, 1, :, :]]
        bank = [b.rearrange("p a t -> p (a t)") for b in bank] + [ps_a[:, :], ps_b[:, :]]

        ld_first, ld_out, ld_mask, ld_gate = (sem(n) for n in ("ld_first", "ld_out", "ld_mask", "ld_gate"))
        ld_x = [sem(f"ld_x{n}") for n in range(NG)]
        ld_ctx = [sem(f"ld_ctx{n}") for n in range(2)]
        ld_w = [sem(f"ld_w{n}") for n in range(WR)]
        st_out = sem("st_out")
        dve_chain, act_chain, pool_set = sem("dve_chain"), sem("act_chain"), sem("pool_set")
        scaled_w = sem("scaled_w")
        stats1, var1, rstd1, ln1 = sem("stats1"), sem("var1"), sem("rstd1"), sem("ln1")
        xn1_turned, xn1_copied = sem("xn1_turned"), sem("xn1_copied")
        v_mm, k_mm, q_mm, r_mm = sem("v_mm"), sem("k_mm"), sem("q_mm"), sem("r_mm")
        v_done, k_done, q_done, r_done = sem("v_done"), sem("k_done"), sem("q_done"), sem("r_done")
        kh_pool, kh_dve, kh_act, res_done, bias_set = sem("kh_pool"), sem("kh_dve"), sem("kh_act"), sem("res_done"), sem("bias_set")
        cur_set, scores, maxed, shift, prob = sem("cur_set"), sem("scores"), sem("maxed"), sem("shift"), sem("prob")
        pt_a, pt_b, pt_copied, pv, o_copied = sem("pt_a"), sem("pt_b"), sem("pt_copied"), sem("pv"), sem("o_copied")
        o_turned, rdened, normed, u_turned, u_copied = (sem(n) for n in ("o_turned", "rdened", "normed", "u_turned", "u_copied"))
        o_mm, x2_done, x2_kept, var2, rstd2, ln2, l_turned, l_copied = (sem(n) for n in (
            "o_mm", "x2_done", "x2_kept", "var2", "rstd2", "ln2", "l_turned", "l_copied"))
        lg_mm, lg_copied, lg_turned, lg_biased, sig_exp = (sem(n) for n in (
            "lg_mm", "lg_copied", "lg_turned", "lg_biased", "sig_exp"))
        h1_mm, h3_mm, silu_done, hid_done, y_mm, y_added = (sem(n) for n in (
            "h1_mm", "h3_mm", "silu_done", "hid_done", "y_mm", "y_added"))

        block = ctx.enter_context(nc.Block())

        def turns(eng, step):
            for k in range(UN):
                step(k, k)
            with eng.Fori(1, NG) as g:
                for r in range(UN):
                    step(g * UN + r, r)
            for k in range(NB, NB + 3):
                step(k, k % UN)

        def on(k, lag):
            return not isinstance(k, int) or 0 <= k - lag < NB

        def after(b, n):
            return not isinstance(b, int) or b >= n

        @block.sync
        def _(sp):
            sp.dma_start(xs[:, 0:UN, :], x[0:UN].rearrange("b t d -> t b d")).then_inc(ld_x[0], 16)
            sp.dma_start(cst[:], consts).then_inc(ld_first, 16)
            sp.dma_start(w_src[:], w_srcT).then_inc(ld_first, 16)
            sp.dma_start(w_tgt[:], w_tgtT).then_inc(ld_first, 16)
            with sp.Fori(0, NG // 2) as i:
                for r in range(2):
                    sp.wait_ge(r_mm, i * 2 + r + 1)
                    sp.dma_start(ctx_r[:, r, :, :], ctxT[:, :, bass.ds((i * 2 + r) * GT, GT)]).then_inc(ld_ctx[r], 16)
            for e in range(WR):
                sp.dma_start(w13[:, e, :, :], w13T[e]).then_inc(ld_w[e], 16)
                sp.dma_start(w2[:, e, :, :], w2T[e]).then_inc(ld_w[e], 16)
            with sp.Fori(1, NE // WR) as i:
                for e in range(WR):
                    sp.wait_ge(y_mm, (i * WR + e - WR + 1) * NG + 1)
                    sp.dma_start(w13[:, e, :, :], w13T[bass.ds(i * WR + e, 1)].rearrange("o p a b -> (o p) a b")).then_inc(ld_w[e], 16)
                    sp.dma_start(w2[:, e, :, :], w2T[bass.ds(i * WR + e, 1)].rearrange("o p a b -> (o p) a b")).then_inc(ld_w[e], 16)
            with sp.Fori(0, NG) as g:
                sp.wait_ge(y_added, g + (NE - 1) * NG + 2)
                sp.dma_start(out[bass.ds(g * UN, UN)].rearrange("b t d -> t b d"), xs[:, bass.ds(g * UN, UN), :]).then_inc(st_out, 16)
            sp.wait_ge(st_out, 16 * NG)

        @block.scalar
        def _(act):
            act.dma_start(mask_b[:], mask.partition_broadcast(P)).then_inc(ld_mask, 16)
            act.dma_start(b_key[:], b_src[0:D].rearrange("(p o) -> p o", o=1)).then_inc(ld_mask, 16)
            act.dma_start(b_qry[:], b_tgt.rearrange("(p o) -> p o", o=1)).then_inc(ld_mask, 16)
            act.dma_start(mask_t[:], maskT).then_inc(ld_mask, 16)
            act.dma_start(b_val[:], b_src[D:2 * D].partition_broadcast(P)).then_inc(ld_mask, 16)
            act.dma_start(gates[:], g2.partition_broadcast(P)).then_inc(ld_out, 16)
            act.dma_start(w_out[:], w_outT).then_inc(ld_out, 16)
            act.dma_start(b_res[:], b_out.partition_broadcast(P)).then_inc(ld_out, 16)
            for n in range(1, NG):
                act.dma_start(xs[:, n * UN:(n + 1) * UN, :], x[n * UN:(n + 1) * UN].rearrange("b t d -> t b d")).then_inc(ld_x[n], 16)
            act.dma_start(gate_w[:], gateT).then_inc(ld_gate, 16)
            act.dma_start(gate_bb[:], gate_b.partition_broadcast(P)).then_inc(ld_gate, 16)

            act.wait_ge(ld_out, 3 * 16)
            nc.scalar.activation(tgates[:], gates[:], ACT.Tanh).then_inc(act_chain, 1)
            act.wait_ge(act_chain, 1)
            nc.scalar.activation(w_outg[:], w_out[:], ACT.Copy, scale=tgates[:, 0:1]).then_inc(scaled_w, 1)
            nc.scalar.activation(b_resg[:], b_res[:], ACT.Copy, scale=tgates[:, 0:1]).then_inc(scaled_w, 1)

            act.wait_ge(ld_first, 3 * 16)
            with act.Fori(0, NG // 2) as i:
                for r in range(2):
                    j = i * 2 + r
                    act.wait_ge(xn1_turned, j + 1)
                    act.wait_ge(r_mm, j + 1)
                    nc.scalar.copy(xn1T[:, r, :], ps_a[:, :]).then_inc(xn1_copied, 1)
                    act.wait_ge(k_done, j + 2)
                    for h in range(KH_DVE, H):
                        last = nc.scalar.activation(kheads[:, h, bass.ds(j * GT, GT)], kT[:, r, :], ACT.Copy,
                                                    scale=head_rows[:, h:h + 1])
                    last.then_inc(kh_act, 1)

            def step(k, r):
                if on(k, 1):
                    b, q = k - 1, (r - 1) % 2
                    if after(b, 2):
                        act.wait_ge(pv, b - 1)
                    act.wait_ge(pt_a, b + 1)
                    nc.scalar.copy(probsT[:, q, 0:UN, :], pt_ps[:, 0, :, :]).then_inc(pt_copied, 1)
                    act.wait_ge(pt_b, b + 1)
                    nc.scalar.copy(probsT[:, q, UN:H, :], pt_ps[:, 1, :, :]).then_inc(pt_copied, 1)
                if on(k, 3):
                    b = k - 3
                    act.wait_ge(l_turned, b + 1)
                    nc.scalar.copy(xn2T[:, bass.ds(b * P, P)], ps_a[:, 0:P]).then_inc(l_copied, 1)
                if on(k, 2):
                    b = k - 2
                    act.wait_ge(u_turned, b + 1)
                    if after(b, 2):
                        act.wait_ge(o_mm, b - 1)
                    nc.scalar.copy(updT[:, r % 2, :], ps_b[:, 0:P]).then_inc(u_copied, 1)
                if on(k, 1):
                    b = k - 1
                    act.wait_ge(pv, b + 1)
                    if after(b, 2):
                        act.wait_ge(o_turned, b - 1)
                    nc.scalar.copy(oT[:, (r - 1) % 2, :, :], ps_a[:, 0:2 * P].rearrange("p (a t) -> p a t", a=2)).then_inc(o_copied, 1)
                if on(k, 0):
                    act.wait_ge(shift, k + 1)
                    if after(k, 2):
                        act.wait_ge(pt_b, k - 1)
                    nc.scalar.activation(probs[:, r % 2, :, :], shifted[:, r % 2, :, :], ACT.Exp, scale=SCALE).then_inc(prob, 1)

            turns(act, step)

            for g in range(NG):
                act.wait_ge(lg_mm, g + 1)
                nc.scalar.copy(lgT[:, g * GT:(g + 1) * GT], bank[g][0:NE, :]).then_inc(lg_copied, 1)
            act.wait_ge(lg_biased, 2)
            nc.scalar.activation(sig[:], z[:], ACT.Exp, scale=-1.0).then_inc(sig_exp, 1)
            nc.scalar.activation(high[:], high[:], ACT.Exp, scale=-1.0).then_inc(sig_exp, 1)

            nc.scalar.preload_act_table(ACT.Silu)
            with act.Fori(0, NE * NG) as u:
                for c, (_, cn) in enumerate(CH):
                    act.wait_ge(h1_mm, u * NC + c + 1)
                    act.wait_ge(hid_done, u * NC + c + 1)
                    nc.scalar.activation(gated[0:cn, c, :], bank[c][0:cn, :], ACT.Silu).then_inc(silu_done, 1)

        @block.gpsimd
        def _(pool):
            nc.gpsimd.memset(minus_half[:], -0.5)
            nc.gpsimd.memset(share[:], 1.0 / P)
            nc.gpsimd.memset(v_cur[:], 0.0).then_inc(pool_set, 1)
            pool.wait_ge(pool_set, 1)

            pool.wait_ge(ld_first, 3 * 16)
            pool.wait_ge(scaled_w, 2)
            for j in range(NG):
                here = slice(j * UN, (j + 1) * UN)
                pool.wait_ge(var1, j + 1)
                nc.gpsimd.tensor_tensor(rs1[:, here], ve1[:, here], minus_half[:], ALU.pow).then_inc(rstd1, 1)
            with pool.Fori(0, NG // 2) as i:
                for r in range(2):
                    j = i * 2 + r
                    pool.wait_ge(k_done, j + 2)
                    for h in range(KH_POOL):
                        last = nc.gpsimd.tensor_tensor(kheads[:, h, bass.ds(j * GT, GT)], kT[:, r, :],
                                                       head_rows[:, h:h + 1].to_broadcast([P, GT]), ALU.mult)
                    last.then_inc(kh_pool, 1)
                    pool.wait_ge(r_done, j + 2)
                    here = xs[:, bass.ds(j * UN, UN), :]
                    nc.gpsimd.tensor_tensor(here, here, b_resg[:].unsqueeze(1).to_broadcast([P, UN, D]), ALU.add).then_inc(res_done, 1)

            def step(k, r):
                if on(k, 0):
                    if after(k, UN):
                        pool.wait_ge(pv, k - UN + 1)
                    nc.gpsimd.tensor_copy(q_cur[:, r, :], qT[:, bass.ds(k * P, P)])
                    nc.gpsimd.tensor_tensor(v_cur[:, r, :, 0:HD], vals[:, bass.ds(k, 1), :].rearrange("p o (h d) -> p (o h) d", h=H),
                                            mask_t[:, bass.ds(k, 1)].unsqueeze(1).to_broadcast([P, H, HD]), ALU.mult)
                    nc.gpsimd.tensor_copy(v_cur[:, r, :, HD:HD + 1], live_t[:, bass.ds(k, 1)].unsqueeze(1).to_broadcast([P, H, 1])).then_inc(cur_set, 1)
                if on(k, 3):
                    b, q = k - 3, (r - 3) % 2
                    pool.wait_ge(var2, b + 1)
                    nc.gpsimd.tensor_tensor(rs2[:, q:q + 1], ve2[:, q:q + 1], minus_half[:, 0:1], ALU.pow).then_inc(rstd2, 1)

            pool.wait_ge(v_done, NG + 1)
            pool.wait_ge(q_done, NG + 1)
            pool.wait_ge(bias_set, 2)
            turns(pool, step)

        @block.vector
        def _(dve):
            links = [0]

            def link(ins):
                links[0] += 1
                ins.then_inc(dve_chain, 1)
                dve.wait_ge(dve_chain, links[0])

            for s, places in ((v_done, 1), (k_done, 1), (q_done, 1), (r_done, 1), (xn1_copied, 1), (kh_pool, 2), (kh_act, 2),
                              (y_mm, 1), (y_added, 1)):
                dve.sem_inc(s, places)
            nc.vector.memset(high[:, NB * NE:NB * NE + 1], KNEE).then_inc(r_mm, 2)

            for j in range(NG):
                dve.wait_ge(ld_x[j], 16)
                for b in range(j * UN, (j + 1) * UN):
                    nc.vector.bn_stats(st1[:, b, :], xs[:, b, :]).then_inc(stats1, 1)
                dve.wait_ge(stats1, (j + 1) * UN)
                for b in range(j * UN, (j + 1) * UN):
                    last = nc.vector.bn_aggr(mv1[:, b, :], st1[:, b, :])
                link(last)
                here = slice(j * UN, (j + 1) * UN)
                nc.vector.tensor_scalar(ve1[:, here], mv1[:, here, 1], LN_EPS, None, ALU.add).then_inc(var1, 1)

            with dve.Fori(0, NG // 2) as i:
                for r in range(2):
                    j = i * 2 + r
                    dve.wait_ge(rstd1, j + 1)
                    dve.wait_ge(r_mm, j + 1)
                    for b in range(UN):
                        last = nc.vector.tensor_scalar(xn1[:, r, b, :], xs[:, bass.ds(j * UN + b, 1), :].rearrange("p o d -> p (o d)"),
                                                       mv1[:, bass.ds(j * UN + b, 1), 0:1].rearrange("p o c -> p (o c)"), rs1[:, bass.ds(j * UN + b, 1)], ALU.subtract, ALU.mult)
                    last.then_inc(ln1, 1)
                    if r == 0:
                        dve.wait_ge(ld_mask, 5 * 16)
                    here, cols = bass.ds(j * UN, UN), bass.ds(j * GT, GT)
                    dve.wait_ge(v_mm, j + 1)
                    nc.vector.tensor_tensor(vals[:, here, :], bank[0].rearrange("p (b d) -> p b d", b=UN),
                                            b_val[:].unsqueeze(1).to_broadcast([P, UN, D]), ALU.add).then_inc(v_done, 1)
                    dve.wait_ge(k_mm, j + 1)
                    dve.wait_ge(r_mm, j + 1)
                    dve.wait_ge(kh_pool, j + 1)
                    dve.wait_ge(kh_act, j + 1)
                    nc.vector.scalar_tensor_tensor(kT[:, r, :], bank[1], b_key[:, 0:1], mask_b[:, cols], ALU.add, ALU.mult).then_inc(k_done, 1)
                    dve.wait_ge(k_done, j + 2)
                    for h in range(KH_POOL, KH_DVE):
                        last = nc.vector.tensor_scalar(kheads[:, h, bass.ds(j * GT, GT)], kT[:, r, :], head_rows[:, h:h + 1], None, ALU.mult)
                    last.then_inc(kh_dve, 1)
                    dve.wait_ge(q_mm, j + 1)
                    nc.vector.scalar_tensor_tensor(qT[:, cols], bank[2], b_qry[:, 0:1], mask_b[:, cols], ALU.add, ALU.mult).then_inc(q_done, 1)
                    dve.wait_ge(r_mm, j + 3)
                    nc.vector.tensor_tensor(xs[:, here, :], bank[3].rearrange("p (b d) -> p b d", b=UN), xs[:, here, :], ALU.add).then_inc(r_done, 1)
            nc.vector.tensor_scalar(bias_b[:], mask_b[:], 0.0, MASKED, ALU.is_equal, ALU.mult).then_inc(bias_set, 1)
            nc.vector.tensor_scalar(live_t[:], mask_t[:], 0.0, None, ALU.not_equal).then_inc(bias_set, 1)

            def step(k, r):
                if on(k, 2):
                    b, q = k - 2, r % 2
                    dve.wait_ge(o_turned, b + 1)
                    turned = ps_b[:, 0:2 * P].rearrange("p (h c) -> p h c", h=H)
                    nc.vector.reciprocal(rden[:, q, :], turned[:, :, HD]).then_inc(rdened, 1)
                    dve.wait_ge(rdened, b + 1)
                    if after(b, 2):
                        dve.wait_ge(u_turned, b - 1)
                    nc.vector.tensor_tensor(upd[:, q, :].rearrange("p (h d) -> p h d", h=H), turned[:, :, 0:HD],
                                            rden[:, q, :].unsqueeze(2).to_broadcast([P, H, HD]), ALU.mult).then_inc(normed, 1)
                if on(k, 3):
                    b, q = k - 3, (r - 3) % 2
                    dve.wait_ge(rstd2, b + 1)
                    nc.vector.tensor_scalar(xn2[:, q, :], x2[:, q, :], mv2[:, q, 0:1], rs2[:, q:q + 1],
                                            ALU.subtract, ALU.mult).then_inc(ln2, 1)
                if on(k, 0):
                    q = r % 2
                    dve.wait_ge(scores, k + 1)
                    nc.vector.tensor_reduce(mx[:, q, :], score_ps[:, q, :, :], AX.X, ALU.max).then_inc(maxed, 1)
                    dve.wait_ge(maxed, k + 1)
                    if after(k, 2):
                        dve.wait_ge(prob, k - 1)
                    nc.vector.tensor_tensor(shifted[:, q, :, :], score_ps[:, q, :, :], mx[:, q, :].unsqueeze(2).to_broadcast([P, H, P]),
                                            ALU.subtract).then_inc(shift, 1)
                if on(k, 2):
                    b, q = k - 2, r % 2
                    here = xs[:, bass.ds(b, 1), :].rearrange("p o d -> p (o d)")
                    dve.wait_ge(o_mm, b + 1)
                    if after(b, 2):
                        dve.wait_ge(ln2, b - 1)
                    nc.vector.tensor_tensor(x2[:, q, :], ps_b[:, 2 * P:3 * P], here, ALU.add).then_inc(x2_done, 1)
                    dve.wait_ge(x2_done, b * 3 + 1)
                    nc.vector.bn_stats(st2[:, q, :], x2[:, q, :]).then_inc(x2_done, 1)
                    dve.wait_ge(x2_done, b * 3 + 2)
                    nc.vector.tensor_scalar(here, x2[:, q, :], 1.0, None, ALU.mult).then_inc(x2_kept, 1)
                    nc.vector.bn_aggr(mv2[:, q, :], st2[:, q, :]).then_inc(x2_done, 1)
                    dve.wait_ge(x2_done, b * 3 + 3)
                    nc.vector.tensor_scalar(ve2[:, q:q + 1], mv2[:, q, 1:2], LN_EPS, None, ALU.add).then_inc(var2, 1)

            dve.wait_ge(res_done, NG)
            turns(dve, step)

            dve.wait_ge(x2_kept, NB)

            dve.wait_ge(ld_gate, 2 * 16)
            dve.wait_ge(lg_turned, 1)
            logits = bank[4][:, 0:NB * NE].rearrange("p (b e) -> p b e", b=NB)
            high3 = high[:, 0:NB * NE].rearrange("p (b e) -> p b e", b=NB)

            def wide(v):
                return v[:].unsqueeze(2).to_broadcast([P, NB, NE])

            nc.vector.tensor_tensor(z[:], logits, gate_bb[:].unsqueeze(1).to_broadcast([P, NB, NE]), ALU.add).then_inc(lg_biased, 1)
            dve.wait_ge(lg_biased, 1)
            nc.vector.tensor_scalar(high3, z[:], KNEE, None, ALU.max).then_inc(lg_biased, 1)
            link(nc.vector.tensor_scalar(key[:], z[:], FLOOR, KNEE, ALU.max, ALU.min))
            dve.wait_ge(sig_exp, 2)
            nc.vector.tensor_scalar(sig[:], sig[:], 1.0, None, ALU.add)
            link(nc.vector.tensor_scalar(high[:], high[:], 1.0, None, ALU.add))
            nc.vector.reciprocal(sig[:], sig[:])
            link(nc.vector.reciprocal(high[:], high[:]))
            link(nc.vector.tensor_scalar(high3, high3, high[:, NB * NE:NB * NE + 1], STRETCH, ALU.subtract, ALU.mult))
            link(nc.vector.tensor_tensor(key[:], key[:], high3, ALU.add))
            for choice in (one, two):
                link(nc.vector.tensor_reduce(best[:], key[:], AX.X, ALU.max))
                link(nc.vector.tensor_tensor(pick[:], key[:], wide(best), ALU.is_equal))
                link(nc.vector.tensor_tensor(pick[:], pick[:], low_first.unsqueeze(1).to_broadcast([P, NB, NE]), ALU.mult))
                link(nc.vector.tensor_reduce(first[:], pick[:], AX.X, ALU.max))
                link(nc.vector.tensor_tensor(choice[:], pick[:], wide(first), ALU.is_equal))
                if choice is one:
                    link(nc.vector.scalar_tensor_tensor(key[:], one[:], TAKEN, key[:], ALU.mult, ALU.add))
            link(nc.vector.tensor_tensor(one[:], one[:], two[:], ALU.add))
            link(nc.vector.tensor_tensor(cw[:], one[:], sig[:], ALU.mult))
            link(nc.vector.tensor_reduce(total[:], cw[:], AX.X, ALU.add))
            link(nc.vector.tensor_scalar(total[:], total[:], TOP_EPS, None, ALU.add))
            link(nc.vector.reciprocal(total[:], total[:]))
            link(nc.vector.tensor_scalar(total[:], total[:], tgates[:, 1:2], None, ALU.mult))
            link(nc.vector.tensor_tensor(cw[:], cw[:], wide(total), ALU.mult))
            link(nc.vector.memset(first[:], 0.0))
            nc.vector.memset(best[:], 0.0).then_inc(hid_done, NC)

            with dve.Fori(0, NE) as e:
                with dve.Fori(0, NG) as g:
                    for c, (_, cn) in enumerate(CH):
                        n = e * (NG * NC) + g * NC + c
                        dve.wait_ge(silu_done, n + 1)
                        dve.wait_ge(h3_mm, n + 1)
                        dve.wait_ge(y_mm, e * NG + g + 1)
                        nc.vector.tensor_tensor(hidT[0:cn, c, :], gated[0:cn, c, :], bank[NC + c][0:cn, :], ALU.mult).then_inc(hid_done, 1)
                    dve.wait_ge(y_mm, e * NG + g + 2)
                    for b in range(UN):
                        here = xs[:, bass.ds(g * UN + b, 1), :].rearrange("p o d -> p (o d)")
                        weight = cw[:].rearrange("p b e -> p (b e)")[:, bass.ds(g * (UN * NE) + b * NE + e, 1)]
                        last = nc.vector.scalar_tensor_tensor(here, bank[6][:, b * P:(b + 1) * P], weight, here, ALU.mult, ALU.add)
                    last.then_inc(y_added, 1)

        @block.tensor
        def _(pe):
            pe.wait_ge(ld_first, 3 * 16)
            pe.wait_ge(scaled_w, 1)
            with pe.Fori(0, NG // 2) as i:
                for r in range(2):
                    j = i * 2 + r
                    pe.wait_ge(ld_ctx[r], i * 16 + 16)
                    pe.wait_ge(v_done, j + 1)
                    for b in range(UN):
                        for f in range(FC):
                            last = nc.tensor.matmul(bank[0][:, b * P:(b + 1) * P], ctx_r[:, r, f, b * P:(b + 1) * P], w_src[:, f, D:2 * D],
                                                    start=(f == 0), stop=(f == FC - 1))
                    last.then_inc(v_mm, 1)
                    pe.wait_ge(k_done, j + 1)
                    for f in range(FC):
                        last = nc.tensor.matmul(bank[1], w_src[:, f, 0:D], ctx_r[:, r, f, :], start=(f == 0), stop=(f == FC - 1))
                    last.then_inc(k_mm, 1)
                    pe.wait_ge(ln1, j + 1)
                    pe.wait_ge(xn1_copied, j + 1)
                    for b in range(UN):
                        last = nc.tensor.transpose(ps_a[:, b * P:(b + 1) * P], xn1[:, r, b, :], ident)
                    last.then_inc(xn1_turned, 1)
                    pe.wait_ge(xn1_copied, j + 2)
                    pe.wait_ge(q_done, j + 1)
                    nc.tensor.matmul(bank[2], w_tgt[:], xn1T[:, r, :], start=True, stop=True).then_inc(q_mm, 1)
                    pe.wait_ge(r_done, j + 1)
                    for b in range(UN):
                        last = nc.tensor.matmul(bank[3][:, b * P:(b + 1) * P], xn1T[:, r, b * P:(b + 1) * P], w_outg[:, 0, :], start=True, stop=True)
                    last.then_inc(r_mm, 1)

            def step(k, r):
                if on(k, 0):
                    q = r % 2
                    pe.wait_ge(cur_set, k + 1)
                    if after(k, 2):
                        pe.wait_ge(shift, k - 1)
                    for half in range(2):
                        dst = score_ps[:, q, half * UN:(half + 1) * UN, :]
                        nc.tensor.matmul(dst, q_cur[:, r, :], kheads[:, half * UN:(half + 1) * UN, bass.ds(k * P, P)], start=True, stop=False)
                        last = nc.tensor.matmul(dst, share[:], bias_b[:, bass.ds(k * P, P)].unsqueeze(1).to_broadcast([P, UN, P]),
                                                start=False, stop=True)
                    last.then_inc(scores, 1)
                if on(k, 2):
                    b, q = k - 2, r % 2
                    pe.wait_ge(o_copied, b + 1)
                    if after(b, 1):
                        pe.wait_ge(x2_done, (b - 1) * 3 + 1)
                    for a in range(2):
                        last = nc.tensor.transpose(ps_b[:, a * P:(a + 1) * P], oT[:, q, a, :], ident)
                    last.then_inc(o_turned, 1)
                if on(k, 1):
                    b, q = k - 1, (r - 1) % 2
                    pe.wait_ge(prob, b + 1)
                    for half, done in enumerate((pt_a, pt_b)):
                        if after(b, 1):
                            pe.wait_ge(pt_copied, b * 2 - 1 + half)
                        for h in range(UN):
                            last = nc.tensor.transpose(pt_ps[:, half, h, :], probs[:, q, half * UN + h, :], ident)
                        last.then_inc(done, 1)
                if on(k, 3):
                    b, q = k - 3, (r - 3) % 2
                    pe.wait_ge(ln2, b + 1)
                    if isinstance(b, int) and b == NB - 1:
                        pass
                    pe.wait_ge(o_copied, b + 2) if on(k, 2) else None
                    nc.tensor.transpose(ps_a[:, 0:P], xn2[:, q, :], ident).then_inc(l_turned, 1)
                if on(k, 2):
                    b, q = k - 2, r % 2
                    pe.wait_ge(normed, b + 1)
                    nc.tensor.transpose(ps_b[:, 0:P], upd[:, q, :], ident).then_inc(u_turned, 1)
                if on(k, 1):
                    b, q, place = k - 1, (r - 1) % 2, (r - 1) % UN
                    if after(b, 2):
                        pe.wait_ge(l_copied, b - 1)
                    for h in range(H):
                        pe.wait_ge(pt_copied, b * 2 + 1 + h // UN) if h % UN == 0 else None
                        row = HP * (h % UN)
                        last = nc.tensor.matmul(ps_a[row:row + HP, (h // UN) * P:(h // UN + 1) * P], v_cur[:, place, h, :], probsT[:, q, h, :],
                                                start=True, stop=True, tile_position=(0, row))
                    last.then_inc(pv, 1)
                if on(k, 2):
                    b, q = k - 2, r % 2
                    pe.wait_ge(u_copied, b + 1)
                    nc.tensor.matmul(ps_b[:, 2 * P:3 * P], updT[:, q, :], w_outg[:, 1, :], start=True, stop=True).then_inc(o_mm, 1)

            pe.wait_ge(kh_pool, NG + 2)
            pe.wait_ge(kh_dve, NG)
            pe.wait_ge(kh_act, NG + 2)
            pe.wait_ge(bias_set, 2)
            turns(pe, step)

            pe.wait_ge(ld_gate, 2 * 16)
            pe.wait_ge(l_copied, NB)
            for g in range(NG):
                nc.tensor.matmul(bank[g][0:NE, :], gate_w[:], xn2T[:, g * GT:(g + 1) * GT], start=True, stop=True).then_inc(lg_mm, 1)
            pe.wait_ge(lg_copied, NG)
            for b in range(NB):
                last = nc.tensor.transpose(bank[4][:, b * NE:(b + 1) * NE], lgT[:, b * P:(b + 1) * P], ident[0:NE, 0:NE])
            last.then_inc(lg_turned, 1)

            pe.wait_ge(lg_biased, 2)
            with pe.Fori(0, NE // WR) as i:
                for w in range(WR):
                    with pe.Fori(0, NG) as g:
                        pe.wait_ge(ld_w[w], i * 32 + 32)
                        u = i * (WR * NG) + w * NG + g
                        for c, (c0, cn) in enumerate(CH):
                            pe.wait_ge(hid_done, u * NC + c + 1)
                            moving = xn2T[:, bass.ds(g * GT, GT)]
                            nc.tensor.matmul(bank[c][0:cn, :], w13[:, w, 0, c0:c0 + cn], moving, start=True, stop=True).then_inc(h1_mm, 1)
                            nc.tensor.matmul(bank[NC + c][0:cn, :], w13[:, w, 1, c0:c0 + cn], moving, start=True, stop=True).then_inc(h3_mm, 1)
                        pe.wait_ge(y_added, u + 1)
                        for c, (_, cn) in enumerate(CH):
                            pe.wait_ge(hid_done, u * NC + c + 1 + NC)
                            for b in range(UN):
                                last = nc.tensor.matmul(bank[6][:, b * P:(b + 1) * P], hidT[0:cn, c, b * P:(b + 1) * P], w2[0:cn, w, c, :],
                                                        start=(c == 0 and b == 0), stop=(c == NC - 1 and b == UN - 1), skip_group_check=True)
                        last.then_inc(y_mm, 1)


def kernel(x, ctx_2048, mask_BxS2_fk1, g_xattn, g_ffn, L0_xattn_W_src, L0_xattn_b_src, L0_xattn_W_tgt, L0_xattn_b_tgt,
           L0_xattn_W_out, L0_xattn_b_out, L0_ffn_w1, L0_ffn_w2, L0_ffn_w3, L0_ffn_new_w1, L0_ffn_new_w2, L0_ffn_new_w3,
           L0_ffn_gate_weight, L0_ffn_new_gate_weight, L0_ffn_gate_bias):
    import numpy as np
    import concourse.bacc as bacc
    from concourse.bass_utils import run_bass_kernel_spmd

    def split(a):
        return a.reshape(-1, P, a.shape[1]).transpose(1, 0, 2)

    ew1 = np.concatenate([L0_ffn_w1, L0_ffn_new_w1], axis=0)
    ew2 = np.concatenate([L0_ffn_w2, L0_ffn_new_w2], axis=0)
    ew3 = np.concatenate([L0_ffn_w3, L0_ffn_new_w3], axis=0)
    w2_rows = np.zeros((NE, NC * P, D), np.float32)
    w2_rows[:, :HID] = ew2.transpose(0, 2, 1)
    consts = np.zeros((P, NCONST), np.float32)
    consts[:, 0:P] = np.eye(P)
    for p in range(P):
        consts[p, P + p // HD] = 1.0
    consts[:, P + H:] = np.arange(NE, 0, -1)
    arrays = {
        "x": x,
        "ctxT": split(np.asarray(ctx_2048).reshape(NB * P, FC * P).T),
        "mask": np.asarray(mask_BxS2_fk1).reshape(-1),
        "maskT": np.asarray(mask_BxS2_fk1).T,
        "g2": np.concatenate([g_xattn, g_ffn]),
        "consts": consts,
        "w_srcT": split(np.asarray(L0_xattn_W_src).T),
        "b_src": L0_xattn_b_src,
        "w_tgtT": np.asarray(L0_xattn_W_tgt).T,
        "b_tgt": L0_xattn_b_tgt,
        "w_outT": split(np.asarray(L0_xattn_W_out).T),
        "b_out": L0_xattn_b_out,
        "w13T": np.stack([ew1.transpose(0, 2, 1), ew3.transpose(0, 2, 1)], axis=2),
        "w2T": w2_rows.reshape(NE, NC, P, D).transpose(0, 2, 1, 3),
        "gateT": np.concatenate([L0_ffn_gate_weight, L0_ffn_new_gate_weight], axis=0).T,
        "gate_b": np.concatenate([np.zeros(NE - 1, np.float32), L0_ffn_gate_bias]),
    }
    arrays = {"in_" + k: np.ascontiguousarray(v) for k, v in arrays.items()}
    nc = bacc.Bacc("TRN2", target_bir_lowering=False, num_devices=1)
    args = [nc.dram_tensor(k, v.shape, mybir.dt.from_np(v.dtype), kind="ExternalInput").ap() for k, v in arrays.items()]
    out = nc.dram_tensor("out_0", (NB, P, D), F32, kind="ExternalOutput").ap()
    build(nc, *args, out)
    r = run_bass_kernel_spmd(nc, [arrays], core_ids=[0])
    return r.results[0]["out_0"]
```

```python
from contextlib import ExitStack

import concourse.bass as bass
from concourse import mybir

ALU = mybir.AluOpType
ACT = mybir.ActivationFunctionType
AX = mybir.AxisListType
F32 = mybir.dt.float32
BF16 = mybir.dt.bfloat16
I32 = mybir.dt.int32

P = 128
NB = 16
D = 128
FC = 2
H, HD = 8, 16
HP = 32
UN = 4
NG = NB // UN
GT = UN * P
NE, HID = 9, 352
CH = [(0, 128), (128, 128), (256, 96)]
NC = len(CH)
KH_POOL, KH_DVE = 2, 5
NT = 2 * NB + NE - 1
TR = 8
RW = D + 2
C_ID, C_WEIGHT = D, D + 1
NOWHERE = 1 << 20
SCALE = HD ** -0.5
MASKED = -1.0e30
LN_EPS = 1e-5
TOP_EPS = 1e-20
KNEE = 8.0
FLOOR = -88.72
STRETCH = 1024.0
TAKEN = -1.0e6
CONSTS = {"ident": P, "head_rows": H, "low_first": NE, "tile_first": NB, "experts_below": NE * NE, "tiles": NT, "rows_below": P}
NCONST = sum(CONSTS.values())


def build(nc, x, ctxT, mask, maskT, g2, consts, w_srcT, b_src, w_tgtT, b_tgt, w_outT, b_out,
          w13T, w2T, gateT, gate_b, x_rows, y_rows, out):
    with ExitStack() as ctx:
        def sb(name, shape, dt=F32):
            return ctx.enter_context(nc.sbuf_tensor(name, shape, dt))

        def ps(name, shape):
            return ctx.enter_context(nc.psum_tensor(name, shape, F32))

        def sem(name):
            return ctx.enter_context(nc.semaphore(name))

        cst = sb("cst", [P, NCONST])
        at, part = 0, {}
        for name, width in CONSTS.items():
            part[name] = cst[:, at:at + width]
            at += width
        ident, head_rows, low_first = part["ident"], part["head_rows"], part["low_first"]
        gates, tgates = sb("gates", [P, 2]), sb("tgates", [P, 2])
        w_src = sb("w_src", [P, FC, 2 * D])
        w_tgt = sb("w_tgt", [P, D])
        w_out, w_outg = sb("w_out", [P, 2, D]), sb("w_outg", [P, 2, D])
        b_key, b_qry = sb("b_key", [P, 1]), sb("b_qry", [P, 1])
        b_val = sb("b_val", [P, D])
        b_res, b_resg = sb("b_res", [P, D]), sb("b_resg", [P, D])
        mask_t, live_t = sb("mask_t", [P, NB]), sb("live_t", [P, NB])
        stage = sb("stage", [P, 2, NB, RW])
        room = stage[:].rearrange("p c b w -> p (c b w)")
        mask_b = room[:, 0:NB * P]
        bias_b = sb("bias_b", [P, NB * P], BF16)
        share = sb("share", [P, P], BF16)
        minus_half = sb("minus_half", [P, UN])

        xs = sb("xs", [P, NB, D])
        st1, mv1 = sb("st1", [P, NB, 6]), sb("mv1", [P, NB, 2])
        ve1, rs1 = sb("ve1", [P, NB]), sb("rs1", [P, NB])
        xn1, xn1T = sb("xn1", [P, 2, UN, D]), sb("xn1T", [P, 2, GT])
        ctx_r = room[:, NB * P:NB * P + 2 * FC * GT].rearrange("p (r f t) -> p r f t", r=2, f=FC)
        kT = sb("kT", [P, 2, GT])
        qT = sb("qT", [P, NB * P])
        kheads = sb("kheads", [P, H, NB * P])
        vals = sb("vals", [P, NB, D])

        q_cur = sb("q_cur", [P, UN, P])
        v_cur = sb("v_cur", [P, UN, H, HP])
        mx = sb("mx", [P, 2, H])
        shifted, probs = sb("shifted", [P, 2, H, P]), sb("probs", [P, 2, H, P])
        probsT = sb("probsT", [P, 2, H, P])
        oT = sb("oT", [P, 2, 2, P])
        rden, upd, updT = sb("rden", [P, 2, H]), sb("upd", [P, 2, D]), sb("updT", [P, 2, P])
        st2, mv2, ve2, rs2 = sb("st2", [P, 2, 6]), sb("mv2", [P, 2, 2]), sb("ve2", [P, 2]), sb("rs2", [P, 2])
        x2, xn2 = sb("x2", [P, 2, D]), sb("xn2", [P, 2, D])
        xn2T = sb("xn2T", [P, NB * P])

        gate_w, gate_bb = sb("gate_w", [P, NE]), sb("gate_bb", [P, NE])
        lgT = qT[0:NE, :]
        z, sig, key, pick = (sb(n, [P, NB, NE]) for n in ("z", "sig", "key", "pick"))
        one, two, cw = (sb(n, [P, NB, NE]) for n in ("one", "two", "cw"))
        both = sb("both", [P, NB, NE], BF16)
        high = sb("high", [P, NB * NE + 1])
        best, first, total = (sb(n, [P, NB]) for n in ("best", "first", "total"))
        rows_below, ones = sb("rows_below", [P, P], BF16), sb("ones", [P, P], BF16)
        filled, below = sb("filled", [P, NE, NB]), sb("below", [P, NE, NE])
        tiles_of, start, end, first_row = (sb(n, [P, NE]) for n in ("tiles_of", "start", "end", "first_row"))
        slot_f, slot = sb("slot_f", [P, 2, NB]), sb("slot", [P, 2, NB], I32)
        passed, expert_f = sb("passed", [1, NT, NE]), sb("expert_f", [1, NT])
        expert_of = sb("expert_of", [1, NT], I32)
        pad_row = sb("pad_row", [P, RW])
        xg, xgT, ids, no_id = sb("xg", [P, TR, RW]), sb("xgT", [P, 2, P]), sb("ids", [P, TR], I32), sb("no_id", [P, 1], I32)
        flat = [t[:].rearrange("p a h t -> p (a h t)") for t in (shifted, probs)] + [kheads[:].rearrange("p h t -> p (h t)")]
        gated, hid = (flat[0][:, i * 2 * HID:(i + 1) * 2 * HID].rearrange("p (r h) -> p r h", r=2) for i in range(2))
        hidT = flat[1][:, 0:2 * NC * P].rearrange("p (r c t) -> p r c t", r=2, c=NC)
        yt = flat[1][:, 2 * NC * P:2 * NC * P + TR * D].rearrange("p (r d) -> p r d", r=TR)
        n13, n2 = NE * 2 * HID, NE * NC * D
        w13 = flat[2][:, 0:n13].rearrange("p (e a h) -> p e a h", e=NE, a=2)
        w2 = flat[2][:, n13:n13 + n2].rearrange("p (e c d) -> p e c d", e=NE, c=NC)
        ys = flat[2][:, n13 + n2:n13 + n2 + 2 * NB * D].rearrange("p (c b d) -> p c b d", c=2, b=NB)

        score_ps = ps("score_ps", [P, 2, H, P])
        pt_ps = ps("pt_ps", [P, 2, UN, P])
        ps_a, ps_b = ps("ps_a", [P, GT]), ps("ps_b", [P, GT])
        bank = [score_ps[:, i // 2, UN * (i % 2):UN * (i % 2) + UN, :] for i in range(4)]
        bank += [pt_ps[:, 0, :, :], pt_ps[:, 1, :, :]]
        bank = [b.rearrange("p a t -> p (a t)") for b in bank] + [ps_a[:, :], ps_b[:, :]]

        ld_first, ld_out, ld_mask, ld_gate = (sem(n) for n in ("ld_first", "ld_out", "ld_mask", "ld_gate"))
        ld_x = [sem(f"ld_x{n}") for n in range(NG)]
        ld_ctx = [sem(f"ld_ctx{n}") for n in range(2)]
        ld_w13, ld_w2, st_pad, st_rows = sem("ld_w13"), sem("ld_w2"), sem("st_pad"), sem("st_rows")
        ld_tile = [sem(f"ld_tile{n}") for n in range(TR)]
        st_y = [sem(f"st_y{n}") for n in range(TR)]
        ld_y = [sem(f"ld_y{n}") for n in range(NG)]
        st_out = sem("st_out")
        dve_chain, act_chain, pool_set = sem("dve_chain"), sem("act_chain"), sem("pool_set")
        scaled_w = sem("scaled_w")
        stats1, var1, rstd1, ln1 = sem("stats1"), sem("var1"), sem("rstd1"), sem("ln1")
        xn1_turned, xn1_copied = sem("xn1_turned"), sem("xn1_copied")
        v_mm, k_mm, q_mm, r_mm = sem("v_mm"), sem("k_mm"), sem("q_mm"), sem("r_mm")
        v_done, k_done, q_done, r_done = sem("v_done"), sem("k_done"), sem("q_done"), sem("r_done")
        kh_pool, kh_dve, kh_act, res_done, bias_set = sem("kh_pool"), sem("kh_dve"), sem("kh_act"), sem("res_done"), sem("bias_set")
        cur_set, scores, maxed, shift, prob = sem("cur_set"), sem("scores"), sem("maxed"), sem("shift"), sem("prob")
        pt_a, pt_b, pt_copied, pv, o_copied = sem("pt_a"), sem("pt_b"), sem("pt_copied"), sem("pv"), sem("o_copied")
        o_turned, rdened, normed, u_turned, u_copied = (sem(n) for n in ("o_turned", "rdened", "normed", "u_turned", "u_copied"))
        o_mm, x2_done, x2_kept, var2, rstd2, ln2, l_turned, l_copied = (sem(n) for n in (
            "o_mm", "x2_done", "x2_kept", "var2", "rstd2", "ln2", "l_turned", "l_copied"))
        lg_mm, lg_copied, lg_turned, lg_biased, sig_exp = (sem(n) for n in (
            "lg_mm", "lg_copied", "lg_turned", "lg_biased", "sig_exp"))
        ids_copied = sem("ids_copied")
        pad_set, staged, ids_set, chosen, ranked, slots_set, table_set = (sem(n) for n in (
            "pad_set", "staged", "ids_set", "chosen", "ranked", "slots_set", "table_set"))
        x_turned, x_copied, h1_mm, h3_mm, silu_done, hid_done = (sem(n) for n in (
            "x_turned", "x_copied", "h1_mm", "h3_mm", "silu_done", "hid_done"))
        ha_turned, hb_turned, ha_copied, hb_copied, y_mm, y_done, y_added = (sem(n) for n in (
            "ha_turned", "hb_turned", "ha_copied", "hb_copied", "y_mm", "y_done", "y_added"))

        block = ctx.enter_context(nc.Block())

        def turns(eng, step):
            for k in range(UN):
                step(k, k)
            with eng.Fori(1, NG) as g:
                for r in range(UN):
                    step(g * UN + r, r)
            for k in range(NB, NB + 3):
                step(k, k % UN)

        def on(k, lag):
            return not isinstance(k, int) or 0 <= k - lag < NB

        def after(b, n):
            return not isinstance(b, int) or b >= n

        def tile_turns(eng, step):
            for k in range(TR):
                step(k, k, 0)
            with eng.Fori(1, NT // TR) as i:
                for r in range(TR):
                    step(i * TR + r, r, i)
            for k in range(NT, NT + 2):
                step(k, k % TR, k // TR)

        def has(k, lag):
            return not isinstance(k, int) or 0 <= k - lag < NT

        @block.sync
        def _(sp):
            sp.dma_start(xs[:, 0:UN, :], x[0:UN].rearrange("b t d -> t b d")).then_inc(ld_x[0], 16)
            sp.dma_start(cst[:], consts).then_inc(ld_first, 16)
            sp.dma_start(w_src[:], w_srcT).then_inc(ld_first, 16)
            sp.dma_start(w_tgt[:], w_tgtT).then_inc(ld_first, 16)
            with sp.Fori(0, NG // 2) as i:
                for r in range(2):
                    sp.wait_ge(r_mm, i * 2 + r + 1)
                    sp.dma_start(ctx_r[:, r, :, :], ctxT[:, :, bass.ds((i * 2 + r) * GT, GT)]).then_inc(ld_ctx[r], 16)
            sp.wait_ge(pad_set, 2)
            sp.dma_start(x_rows.rearrange("(n p) w -> p n w", p=P), pad_row[:].unsqueeze(1).to_broadcast([P, NT, RW])).then_inc(st_pad, 16)
            sp.wait_ge(scores, NB)
            sp.dma_start(w13, w13T.rearrange("e p a b -> p e a b")).then_inc(ld_w13, 16)
            sp.dma_start(w2, w2T.rearrange("e p a b -> p e a b")).then_inc(ld_w2, 16)

            sp.wait_ge(st_rows, 2 * NB * 16)
            for r in range(TR):
                sp.dma_start(xg[:, r, :], x_rows[r * P:(r + 1) * P]).then_inc(ld_tile[r], 16)
            with sp.Fori(1, NT // TR) as i:
                for r in range(TR):
                    sp.wait_ge(st_y[r], i * 16)
                    sp.dma_start(xg[:, r, :], x_rows[bass.ds((i * TR + r) * P, P)]).then_inc(ld_tile[r], 16)

            for r in range(TR):
                sp.wait_ge(st_y[r], (NT // TR) * 16)
            y_tok = y_rows.rearrange("(c b t) d -> t c b d", c=2, t=P)
            for g in range(NG):
                for c in range(2):
                    sp.dma_start(ys[:, c, g * UN:(g + 1) * UN, :], y_tok[:, c, g * UN:(g + 1) * UN, :]).then_inc(ld_y[g], 16)
            for g in range(NG):
                sp.wait_ge(y_added, 2 * g + 2)
                sp.dma_start(out[g * UN:(g + 1) * UN].rearrange("b t d -> t b d"), xs[:, g * UN:(g + 1) * UN, :]).then_inc(st_out, 16)
            sp.wait_ge(st_out, 16 * NG)

        @block.scalar
        def _(act):
            act.dma_start(mask_b[:], mask.partition_broadcast(P)).then_inc(ld_mask, 16)
            act.dma_start(b_key[:], b_src[0:D].rearrange("(p o) -> p o", o=1)).then_inc(ld_mask, 16)
            act.dma_start(b_qry[:], b_tgt.rearrange("(p o) -> p o", o=1)).then_inc(ld_mask, 16)
            act.dma_start(mask_t[:], maskT).then_inc(ld_mask, 16)
            act.dma_start(b_val[:], b_src[D:2 * D].partition_broadcast(P)).then_inc(ld_mask, 16)
            act.dma_start(gates[:], g2.partition_broadcast(P)).then_inc(ld_out, 16)
            act.dma_start(w_out[:], w_outT).then_inc(ld_out, 16)
            act.dma_start(b_res[:], b_out.partition_broadcast(P)).then_inc(ld_out, 16)
            for n in range(1, NG):
                act.dma_start(xs[:, n * UN:(n + 1) * UN, :], x[n * UN:(n + 1) * UN].rearrange("b t d -> t b d")).then_inc(ld_x[n], 16)
            act.dma_start(gate_w[:], gateT).then_inc(ld_gate, 16)
            act.dma_start(gate_bb[:], gate_b.partition_broadcast(P)).then_inc(ld_gate, 16)

            act.wait_ge(ld_out, 3 * 16)
            nc.scalar.activation(tgates[:], gates[:], ACT.Tanh).then_inc(act_chain, 1)
            act.wait_ge(act_chain, 1)
            nc.scalar.activation(w_outg[:], w_out[:], ACT.Copy, scale=tgates[:, 0:1]).then_inc(scaled_w, 1)
            nc.scalar.activation(b_resg[:], b_res[:], ACT.Copy, scale=tgates[:, 0:1]).then_inc(scaled_w, 1)

            act.wait_ge(ld_first, 3 * 16)
            with act.Fori(0, NG // 2) as i:
                for r in range(2):
                    j = i * 2 + r
                    act.wait_ge(xn1_turned, j + 1)
                    act.wait_ge(r_mm, j + 1)
                    nc.scalar.copy(xn1T[:, r, :], ps_a[:, :]).then_inc(xn1_copied, 1)
                    act.wait_ge(k_done, j + 2)
                    for h in range(KH_DVE, H):
                        last = nc.scalar.activation(kheads[:, h, bass.ds(j * GT, GT)], kT[:, r, :], ACT.Copy,
                                                    scale=head_rows[:, h:h + 1])
                    last.then_inc(kh_act, 1)

            def step(k, r):
                if on(k, 1):
                    b, q = k - 1, (r - 1) % 2
                    if after(b, 2):
                        act.wait_ge(pv, b - 1)
                    act.wait_ge(pt_a, b + 1)
                    nc.scalar.copy(probsT[:, q, 0:UN, :], pt_ps[:, 0, :, :]).then_inc(pt_copied, 1)
                    act.wait_ge(pt_b, b + 1)
                    nc.scalar.copy(probsT[:, q, UN:H, :], pt_ps[:, 1, :, :]).then_inc(pt_copied, 1)
                if on(k, 3):
                    b = k - 3
                    act.wait_ge(l_turned, b + 1)
                    nc.scalar.copy(xn2T[:, bass.ds(b * P, P)], ps_a[:, 0:P]).then_inc(l_copied, 1)
                if on(k, 2):
                    b = k - 2
                    act.wait_ge(u_turned, b + 1)
                    if after(b, 2):
                        act.wait_ge(o_mm, b - 1)
                    nc.scalar.copy(updT[:, r % 2, :], ps_b[:, 0:P]).then_inc(u_copied, 1)
                if on(k, 1):
                    b = k - 1
                    act.wait_ge(pv, b + 1)
                    if after(b, 2):
                        act.wait_ge(o_turned, b - 1)
                    nc.scalar.copy(oT[:, (r - 1) % 2, :, :], ps_a[:, 0:2 * P].rearrange("p (a t) -> p a t", a=2)).then_inc(o_copied, 1)
                if on(k, 0):
                    act.wait_ge(shift, k + 1)
                    if after(k, 2):
                        act.wait_ge(pt_b, k - 1)
                    nc.scalar.activation(probs[:, r % 2, :, :], shifted[:, r % 2, :, :], ACT.Exp, scale=SCALE).then_inc(prob, 1)
                if on(k, 3):
                    b = k - 3
                    act.wait_ge(ln2, b + 1)
                    nc.scalar.copy(stage[:, :, bass.ds(b, 1), 0:D].rearrange("p c o d -> p (c o) d"),
                                   xn2[:, (r - 3) % 2, :].unsqueeze(1).to_broadcast([P, 2, D])).then_inc(staged, 1)

            turns(act, step)

            for g in range(NG):
                act.wait_ge(lg_mm, g + 1)
                nc.scalar.copy(lgT[:, g * GT:(g + 1) * GT], bank[g][0:NE, :]).then_inc(lg_copied, 1)
            act.wait_ge(lg_biased, 2)
            nc.scalar.activation(sig[:], z[:], ACT.Exp, scale=-1.0).then_inc(sig_exp, 1)
            nc.scalar.activation(high[:], high[:], ACT.Exp, scale=-1.0).then_inc(sig_exp, 1)

            nc.scalar.preload_act_table(ACT.Silu)
            act.wait_ge(table_set, 1)

            def tile(k, r, i):
                if has(k, 1):
                    t, q = k - 1, (r - 1) % 2
                    act.wait_ge(h1_mm, t + 1)
                    if not isinstance(t, int) or t >= 2:
                        act.wait_ge(hid_done, t - 1)
                    nc.scalar.activation(gated[:, q, :], bank[q][:, 0:HID], ACT.Silu).then_inc(silu_done, 1)
                if has(k, 2):
                    t, q = k - 2, r % 2
                    act.wait_ge(ha_turned, t + 1)
                    if not isinstance(t, int) or t >= 2:
                        act.wait_ge(y_mm, t - 1)
                    nc.scalar.copy(hidT[:, q, 0:2, :], bank[4][:, 0:2 * P].rearrange("p (c t) -> p c t", c=2)).then_inc(ha_copied, 1)
                if has(k, 0):
                    act.wait_ge(x_turned, k + 1)
                    if not isinstance(k, int) or k >= 2:
                        act.wait_ge(h3_mm, k - 1)
                    nc.scalar.copy(xgT[:, r % 2, :], bank[6][:, 0:P]).then_inc(x_copied, 1)

            tile_turns(act, tile)

        @block.gpsimd
        def _(pool):
            nc.gpsimd.memset(minus_half[:], -0.5)
            nc.gpsimd.memset(share[:], 1.0 / P)
            nc.gpsimd.memset(no_id[:], 0)
            nc.gpsimd.memset(ones[:], 1.0)
            nc.gpsimd.memset(pad_row[:], 0.0).then_inc(pad_set, 1)
            pool.wait_ge(pad_set, 1)
            nc.gpsimd.iota(pad_row[:, C_ID:C_ID + 1].bitcast(I32), pattern=[[0, 1]], base=NOWHERE, channel_multiplier=1).then_inc(pad_set, 1)
            nc.gpsimd.memset(v_cur[:], 0.0).then_inc(pool_set, 1)
            pool.wait_ge(pool_set, 1)

            pool.wait_ge(ld_first, 3 * 16)
            pool.wait_ge(scaled_w, 2)
            for j in range(NG):
                here = slice(j * UN, (j + 1) * UN)
                pool.wait_ge(var1, j + 1)
                nc.gpsimd.tensor_tensor(rs1[:, here], ve1[:, here], minus_half[:], ALU.pow).then_inc(rstd1, 1)
            with pool.Fori(0, NG // 2) as i:
                for r in range(2):
                    j = i * 2 + r
                    pool.wait_ge(k_done, j + 2)
                    for h in range(KH_POOL):
                        last = nc.gpsimd.tensor_tensor(kheads[:, h, bass.ds(j * GT, GT)], kT[:, r, :],
                                                       head_rows[:, h:h + 1].to_broadcast([P, GT]), ALU.mult)
                    last.then_inc(kh_pool, 1)
                    pool.wait_ge(r_done, j + 2)
                    here = xs[:, bass.ds(j * UN, UN), :]
                    nc.gpsimd.tensor_tensor(here, here, b_resg[:].unsqueeze(1).to_broadcast([P, UN, D]), ALU.add).then_inc(res_done, 1)

            def step(k, r):
                if on(k, 0):
                    if after(k, UN):
                        pool.wait_ge(pv, k - UN + 1)
                    nc.gpsimd.tensor_copy(q_cur[:, r, :], qT[:, bass.ds(k * P, P)])
                    nc.gpsimd.tensor_tensor(v_cur[:, r, :, 0:HD], vals[:, bass.ds(k, 1), :].rearrange("p o (h d) -> p (o h) d", h=H),
                                            mask_t[:, bass.ds(k, 1)].unsqueeze(1).to_broadcast([P, H, HD]), ALU.mult)
                    nc.gpsimd.tensor_copy(v_cur[:, r, :, HD:HD + 1], live_t[:, bass.ds(k, 1)].unsqueeze(1).to_broadcast([P, H, 1])).then_inc(cur_set, 1)
                if on(k, 3):
                    b, q = k - 3, (r - 3) % 2
                    pool.wait_ge(var2, b + 1)
                    nc.gpsimd.tensor_tensor(rs2[:, q:q + 1], ve2[:, q:q + 1], minus_half[:, 0:1], ALU.pow).then_inc(rstd2, 1)

            pool.wait_ge(v_done, NG + 1)
            pool.wait_ge(q_done, NG + 1)
            pool.wait_ge(bias_set, 2)
            turns(pool, step)

            pool.wait_ge(staged, NB)
            nc.gpsimd.iota(stage[:, :, :, C_ID:C_ID + 1].bitcast(I32).rearrange("p c b o -> p (c b o)"), pattern=[[P, 2 * NB]], base=0, channel_multiplier=1).then_inc(ids_set, 1)
            pool.wait_ge(ids_set, 1)
            pool.wait_ge(st_pad, 16)
            pool.wait_ge(slots_set, 2)
            for c in range(2):
                for b in range(NB):
                    pool.indirect_dma_start(x_rows[:, :], bass.IndirectOffsetOnAxis(ap=slot[:, c, b:b + 1], axis=0), stage[:, c, b, :], None,
                                            bounds_check=NT * P - 1, oob_is_err=False).then_inc(st_rows, 16)

            last_row = pool.to_reg(2 * NB * P - 1)

            def tile(k, r, i):
                if has(k, 0):
                    if has(k, 1):
                        pool.wait_ge(ids_copied, k)
                    pool.wait_ge(y_done, k + 1)
                    nc.gpsimd.tensor_tensor(ids[:, r:r + 1], xg[:, r, C_ID:C_ID + 1].bitcast(I32), no_id[:], ALU.add).then_inc(ids_copied, 1)
                if has(k, 1):
                    place = (r - 1) % TR
                    if isinstance(k, int) and k == NT:
                        pool.wait_ge(ids_copied, NT)
                    pool.indirect_dma_start(y_rows[:, :], bass.IndirectOffsetOnAxis(ap=ids[:, place:place + 1], axis=0), yt[:, place, :], None,
                                            bounds_check=last_row, oob_is_err=False).then_inc(st_y[place], 16)

            tile_turns(pool, tile)

        @block.vector
        def _(dve):
            links = [0]

            def link(ins):
                links[0] += 1
                ins.then_inc(dve_chain, 1)
                dve.wait_ge(dve_chain, links[0])

            for s, places in ((v_done, 1), (k_done, 1), (q_done, 1), (r_done, 1), (xn1_copied, 1), (kh_pool, 2), (kh_act, 2),
                              ):
                dve.sem_inc(s, places)
            nc.vector.memset(high[:, NB * NE:NB * NE + 1], KNEE).then_inc(r_mm, 2)

            for j in range(NG):
                dve.wait_ge(ld_x[j], 16)
                for b in range(j * UN, (j + 1) * UN):
                    nc.vector.bn_stats(st1[:, b, :], xs[:, b, :]).then_inc(stats1, 1)
                dve.wait_ge(stats1, (j + 1) * UN)
                for b in range(j * UN, (j + 1) * UN):
                    last = nc.vector.bn_aggr(mv1[:, b, :], st1[:, b, :])
                link(last)
                here = slice(j * UN, (j + 1) * UN)
                nc.vector.tensor_scalar(ve1[:, here], mv1[:, here, 1], LN_EPS, None, ALU.add).then_inc(var1, 1)

            with dve.Fori(0, NG // 2) as i:
                for r in range(2):
                    j = i * 2 + r
                    dve.wait_ge(rstd1, j + 1)
                    dve.wait_ge(r_mm, j + 1)
                    for b in range(UN):
                        last = nc.vector.tensor_scalar(xn1[:, r, b, :], xs[:, bass.ds(j * UN + b, 1), :].rearrange("p o d -> p (o d)"),
                                                       mv1[:, bass.ds(j * UN + b, 1), 0:1].rearrange("p o c -> p (o c)"), rs1[:, bass.ds(j * UN + b, 1)], ALU.subtract, ALU.mult)
                    last.then_inc(ln1, 1)
                    if r == 0:
                        dve.wait_ge(ld_mask, 5 * 16)
                    here, cols = bass.ds(j * UN, UN), bass.ds(j * GT, GT)
                    dve.wait_ge(v_mm, j + 1)
                    nc.vector.tensor_tensor(vals[:, here, :], bank[0].rearrange("p (b d) -> p b d", b=UN),
                                            b_val[:].unsqueeze(1).to_broadcast([P, UN, D]), ALU.add).then_inc(v_done, 1)
                    dve.wait_ge(k_mm, j + 1)
                    dve.wait_ge(r_mm, j + 1)
                    dve.wait_ge(kh_pool, j + 1)
                    dve.wait_ge(kh_act, j + 1)
                    nc.vector.scalar_tensor_tensor(kT[:, r, :], bank[1], b_key[:, 0:1], mask_b[:, cols], ALU.add, ALU.mult).then_inc(k_done, 1)
                    dve.wait_ge(k_done, j + 2)
                    for h in range(KH_POOL, KH_DVE):
                        last = nc.vector.tensor_scalar(kheads[:, h, bass.ds(j * GT, GT)], kT[:, r, :], head_rows[:, h:h + 1], None, ALU.mult)
                    last.then_inc(kh_dve, 1)
                    dve.wait_ge(q_mm, j + 1)
                    nc.vector.scalar_tensor_tensor(qT[:, cols], bank[2], b_qry[:, 0:1], mask_b[:, cols], ALU.add, ALU.mult).then_inc(q_done, 1)
                    dve.wait_ge(r_mm, j + 3)
                    nc.vector.tensor_tensor(xs[:, here, :], bank[3].rearrange("p (b d) -> p b d", b=UN), xs[:, here, :], ALU.add).then_inc(r_done, 1)
            nc.vector.tensor_scalar(bias_b[:], mask_b[:], 0.0, MASKED, ALU.is_equal, ALU.mult).then_inc(bias_set, 1)
            nc.vector.tensor_copy(rows_below[:], part["rows_below"])
            nc.vector.tensor_scalar(live_t[:], mask_t[:], 0.0, None, ALU.not_equal).then_inc(bias_set, 1)

            def step(k, r):
                if on(k, 2):
                    b, q = k - 2, r % 2
                    dve.wait_ge(o_turned, b + 1)
                    turned = ps_b[:, 0:2 * P].rearrange("p (h c) -> p h c", h=H)
                    nc.vector.reciprocal(rden[:, q, :], turned[:, :, HD]).then_inc(rdened, 1)
                    dve.wait_ge(rdened, b + 1)
                    if after(b, 2):
                        dve.wait_ge(u_turned, b - 1)
                    nc.vector.tensor_tensor(upd[:, q, :].rearrange("p (h d) -> p h d", h=H), turned[:, :, 0:HD],
                                            rden[:, q, :].unsqueeze(2).to_broadcast([P, H, HD]), ALU.mult).then_inc(normed, 1)
                if on(k, 3):
                    b, q = k - 3, (r - 3) % 2
                    dve.wait_ge(rstd2, b + 1)
                    if after(b, 2):
                        dve.wait_ge(staged, b - 1)
                    nc.vector.tensor_scalar(xn2[:, q, :], x2[:, q, :], mv2[:, q, 0:1], rs2[:, q:q + 1],
                                            ALU.subtract, ALU.mult).then_inc(ln2, 1)
                if on(k, 0):
                    q = r % 2
                    dve.wait_ge(scores, k + 1)
                    nc.vector.tensor_reduce(mx[:, q, :], score_ps[:, q, :, :], AX.X, ALU.max).then_inc(maxed, 1)
                    dve.wait_ge(maxed, k + 1)
                    if after(k, 2):
                        dve.wait_ge(prob, k - 1)
                    nc.vector.tensor_tensor(shifted[:, q, :, :], score_ps[:, q, :, :], mx[:, q, :].unsqueeze(2).to_broadcast([P, H, P]),
                                            ALU.subtract).then_inc(shift, 1)
                if on(k, 2):
                    b, q = k - 2, r % 2
                    here = xs[:, bass.ds(b, 1), :].rearrange("p o d -> p (o d)")
                    dve.wait_ge(o_mm, b + 1)
                    if after(b, 2):
                        dve.wait_ge(ln2, b - 1)
                    nc.vector.tensor_tensor(x2[:, q, :], ps_b[:, 2 * P:3 * P], here, ALU.add).then_inc(x2_done, 1)
                    dve.wait_ge(x2_done, b * 3 + 1)
                    nc.vector.bn_stats(st2[:, q, :], x2[:, q, :]).then_inc(x2_done, 1)
                    dve.wait_ge(x2_done, b * 3 + 2)
                    nc.vector.tensor_scalar(here, x2[:, q, :], 1.0, None, ALU.mult).then_inc(x2_kept, 1)
                    nc.vector.bn_aggr(mv2[:, q, :], st2[:, q, :]).then_inc(x2_done, 1)
                    dve.wait_ge(x2_done, b * 3 + 3)
                    nc.vector.tensor_scalar(ve2[:, q:q + 1], mv2[:, q, 1:2], LN_EPS, None, ALU.add).then_inc(var2, 1)

            dve.wait_ge(res_done, NG)
            turns(dve, step)

            dve.wait_ge(x2_kept, NB)

            dve.wait_ge(ld_gate, 2 * 16)
            dve.wait_ge(lg_turned, 1)
            logits = bank[4][:, 0:NB * NE].rearrange("p (b e) -> p b e", b=NB)
            high3 = high[:, 0:NB * NE].rearrange("p (b e) -> p b e", b=NB)

            def wide(v):
                return v[:].unsqueeze(2).to_broadcast([P, NB, NE])

            nc.vector.tensor_tensor(z[:], logits, gate_bb[:].unsqueeze(1).to_broadcast([P, NB, NE]), ALU.add).then_inc(lg_biased, 1)
            dve.wait_ge(lg_biased, 1)
            nc.vector.tensor_scalar(high3, z[:], KNEE, None, ALU.max).then_inc(lg_biased, 1)
            link(nc.vector.tensor_scalar(key[:], z[:], FLOOR, KNEE, ALU.max, ALU.min))
            dve.wait_ge(sig_exp, 2)
            nc.vector.tensor_scalar(sig[:], sig[:], 1.0, None, ALU.add)
            link(nc.vector.tensor_scalar(high[:], high[:], 1.0, None, ALU.add))
            nc.vector.reciprocal(sig[:], sig[:])
            link(nc.vector.reciprocal(high[:], high[:]))
            link(nc.vector.tensor_scalar(high3, high3, high[:, NB * NE:NB * NE + 1], STRETCH, ALU.subtract, ALU.mult))
            link(nc.vector.tensor_tensor(key[:], key[:], high3, ALU.add))
            for choice in (one, two):
                link(nc.vector.tensor_reduce(best[:], key[:], AX.X, ALU.max))
                link(nc.vector.tensor_tensor(pick[:], key[:], wide(best), ALU.is_equal))
                link(nc.vector.tensor_tensor(pick[:], pick[:], low_first.unsqueeze(1).to_broadcast([P, NB, NE]), ALU.mult))
                link(nc.vector.tensor_reduce(first[:], pick[:], AX.X, ALU.max))
                link(nc.vector.tensor_tensor(choice[:], pick[:], wide(first), ALU.is_equal))
                if choice is one:
                    link(nc.vector.scalar_tensor_tensor(key[:], one[:], TAKEN, key[:], ALU.mult, ALU.add))
            nc.vector.tensor_tensor(both[:], one[:], two[:], ALU.add).then_inc(chosen, 1)
            dve.wait_ge(chosen, 1)
            link(nc.vector.tensor_tensor(cw[:], both[:], sig[:], ALU.mult))
            link(nc.vector.tensor_reduce(total[:], cw[:], AX.X, ALU.add))
            link(nc.vector.tensor_scalar(total[:], total[:], TOP_EPS, None, ALU.add))
            link(nc.vector.reciprocal(total[:], total[:]))
            link(nc.vector.tensor_scalar(total[:], total[:], tgates[:, 1:2], None, ALU.mult))
            link(nc.vector.tensor_tensor(cw[:], cw[:], wide(total), ALU.mult))
            dve.wait_ge(staged, NB)
            for c, choice in enumerate((one, two)):
                link(nc.vector.tensor_tensor(pick[:], choice[:], cw[:], ALU.mult))
                link(nc.vector.tensor_reduce(stage[:, c, :, C_WEIGHT], pick[:], AX.X, ALU.add))

            dve.wait_ge(ranked, 2)
            rank = bank[5][:, 0:NB * NE].rearrange("p (b e) -> p b e", b=NB)
            link(nc.vector.tensor_tensor(filled[:], bank[6][:, 0:NE].unsqueeze(2).to_broadcast([P, NE, NB]),
                                         part["tile_first"].unsqueeze(1).to_broadcast([P, NE, NB]), ALU.is_gt))
            link(nc.vector.tensor_reduce(tiles_of[:], filled[:], AX.X, ALU.add))
            link(nc.vector.tensor_tensor(below[:], part["experts_below"].rearrange("p (e f) -> p e f", e=NE),
                                         tiles_of[:].unsqueeze(1).to_broadcast([P, NE, NE]), ALU.mult))
            link(nc.vector.tensor_reduce(start[:], below[:], AX.X, ALU.add))
            nc.vector.tensor_tensor(end[:], start[:], tiles_of[:], ALU.add)
            link(nc.vector.tensor_scalar(first_row[:], start[:], float(P), None, ALU.mult))
            link(nc.vector.tensor_tensor(key[:], rank, first_row[:].unsqueeze(1).to_broadcast([P, NB, NE]), ALU.add))
            for c, choice in enumerate((one, two)):
                link(nc.vector.tensor_tensor(pick[:], choice[:], key[:], ALU.mult))
                link(nc.vector.tensor_reduce(slot_f[:, c, :], pick[:], AX.X, ALU.add))
                nc.vector.tensor_copy(slot[:, c, :], slot_f[:, c, :]).then_inc(slots_set, 1)
            link(nc.vector.tensor_tensor(passed[:], part["tiles"][0:1].unsqueeze(2).to_broadcast([1, NT, NE]),
                                         end[0:1].unsqueeze(1).to_broadcast([1, NT, NE]), ALU.is_ge))
            link(nc.vector.tensor_reduce(expert_f[:], passed[:], AX.X, ALU.add))
            nc.vector.tensor_scalar(expert_of[:], expert_f[:], NE - 1.0, None, ALU.min).then_inc(table_set, 1)

            def tile(k, r, i):
                if has(k, 2):
                    t, q = k - 2, r % 2
                    dve.wait_ge(hb_turned, t + 1)
                    if not isinstance(t, int) or t >= 2:
                        dve.wait_ge(y_mm, t - 1)
                    n = CH[2][1]
                    nc.vector.tensor_copy(hidT[0:n, q, 2, :], bank[5][0:n, 0:P]).then_inc(hb_copied, 1)
                if has(k, 1):
                    t, q = k - 1, (r - 1) % 2
                    dve.wait_ge(silu_done, t + 1)
                    dve.wait_ge(h3_mm, t + 1)
                    if not isinstance(t, int) or t >= 2:
                        dve.wait_ge(hb_turned, t - 1)
                    nc.vector.tensor_tensor(hid[:, q, :], gated[:, q, :], bank[2 + q][:, 0:HID], ALU.mult).then_inc(hid_done, 1)
                if has(k, 2):
                    t, place = k - 2, (r - 2) % TR
                    turn = i if r >= 2 else i - 1
                    dve.wait_ge(y_mm, t + 1)
                    if not isinstance(k, int) or t >= TR:
                        dve.wait_ge(st_y[place], turn * 16)
                    nc.vector.tensor_scalar(yt[:, place, :], bank[7][:, 0:D], xg[:, place, C_WEIGHT:C_WEIGHT + 1], None, ALU.mult).then_inc(y_done, 1)

            tile_turns(dve, tile)

            for g in range(NG):
                here = slice(g * UN, (g + 1) * UN)
                dve.wait_ge(ld_y[g], 2 * 16)
                for c in range(2):
                    nc.vector.tensor_tensor(xs[:, here, :], xs[:, here, :], ys[:, c, here, :], ALU.add).then_inc(y_added, 1)
                    dve.wait_ge(y_added, 2 * g + c + 1)

        @block.tensor
        def _(pe):
            pe.wait_ge(ld_first, 3 * 16)
            pe.wait_ge(scaled_w, 1)
            with pe.Fori(0, NG // 2) as i:
                for r in range(2):
                    j = i * 2 + r
                    pe.wait_ge(ld_ctx[r], i * 16 + 16)
                    pe.wait_ge(v_done, j + 1)
                    for b in range(UN):
                        for f in range(FC):
                            last = nc.tensor.matmul(bank[0][:, b * P:(b + 1) * P], ctx_r[:, r, f, b * P:(b + 1) * P], w_src[:, f, D:2 * D],
                                                    start=(f == 0), stop=(f == FC - 1))
                    last.then_inc(v_mm, 1)
                    pe.wait_ge(k_done, j + 1)
                    for f in range(FC):
                        last = nc.tensor.matmul(bank[1], w_src[:, f, 0:D], ctx_r[:, r, f, :], start=(f == 0), stop=(f == FC - 1))
                    last.then_inc(k_mm, 1)
                    pe.wait_ge(ln1, j + 1)
                    pe.wait_ge(xn1_copied, j + 1)
                    for b in range(UN):
                        last = nc.tensor.transpose(ps_a[:, b * P:(b + 1) * P], xn1[:, r, b, :], ident)
                    last.then_inc(xn1_turned, 1)
                    pe.wait_ge(xn1_copied, j + 2)
                    pe.wait_ge(q_done, j + 1)
                    nc.tensor.matmul(bank[2], w_tgt[:], xn1T[:, r, :], start=True, stop=True).then_inc(q_mm, 1)
                    pe.wait_ge(r_done, j + 1)
                    for b in range(UN):
                        last = nc.tensor.matmul(bank[3][:, b * P:(b + 1) * P], xn1T[:, r, b * P:(b + 1) * P], w_outg[:, 0, :], start=True, stop=True)
                    last.then_inc(r_mm, 1)

            def step(k, r):
                if on(k, 0):
                    q = r % 2
                    pe.wait_ge(cur_set, k + 1)
                    if after(k, 2):
                        pe.wait_ge(shift, k - 1)
                    for half in range(2):
                        dst = score_ps[:, q, half * UN:(half + 1) * UN, :]
                        nc.tensor.matmul(dst, q_cur[:, r, :], kheads[:, half * UN:(half + 1) * UN, bass.ds(k * P, P)], start=True, stop=False)
                        last = nc.tensor.matmul(dst, share[:], bias_b[:, bass.ds(k * P, P)].unsqueeze(1).to_broadcast([P, UN, P]),
                                                start=False, stop=True)
                    last.then_inc(scores, 1)
                if on(k, 2):
                    b, q = k - 2, r % 2
                    pe.wait_ge(o_copied, b + 1)
                    if after(b, 1):
                        pe.wait_ge(x2_done, (b - 1) * 3 + 1)
                    for a in range(2):
                        last = nc.tensor.transpose(ps_b[:, a * P:(a + 1) * P], oT[:, q, a, :], ident)
                    last.then_inc(o_turned, 1)
                if on(k, 1):
                    b, q = k - 1, (r - 1) % 2
                    pe.wait_ge(prob, b + 1)
                    for half, done in enumerate((pt_a, pt_b)):
                        if after(b, 1):
                            pe.wait_ge(pt_copied, b * 2 - 1 + half)
                        for h in range(UN):
                            last = nc.tensor.transpose(pt_ps[:, half, h, :], probs[:, q, half * UN + h, :], ident)
                        last.then_inc(done, 1)
                if on(k, 3):
                    b, q = k - 3, (r - 3) % 2
                    pe.wait_ge(ln2, b + 1)
                    if isinstance(b, int) and b == NB - 1:
                        pass
                    pe.wait_ge(o_copied, b + 2) if on(k, 2) else None
                    nc.tensor.transpose(ps_a[:, 0:P], xn2[:, q, :], ident).then_inc(l_turned, 1)
                if on(k, 2):
                    b, q = k - 2, r % 2
                    pe.wait_ge(normed, b + 1)
                    nc.tensor.transpose(ps_b[:, 0:P], upd[:, q, :], ident).then_inc(u_turned, 1)
                if on(k, 1):
                    b, q, place = k - 1, (r - 1) % 2, (r - 1) % UN
                    if after(b, 2):
                        pe.wait_ge(l_copied, b - 1)
                    for h in range(H):
                        pe.wait_ge(pt_copied, b * 2 + 1 + h // UN) if h % UN == 0 else None
                        row = HP * (h % UN)
                        last = nc.tensor.matmul(ps_a[row:row + HP, (h // UN) * P:(h // UN + 1) * P], v_cur[:, place, h, :], probsT[:, q, h, :],
                                                start=True, stop=True, tile_position=(0, row))
                    last.then_inc(pv, 1)
                if on(k, 2):
                    b, q = k - 2, r % 2
                    pe.wait_ge(u_copied, b + 1)
                    nc.tensor.matmul(ps_b[:, 2 * P:3 * P], updT[:, q, :], w_outg[:, 1, :], start=True, stop=True).then_inc(o_mm, 1)

            pe.wait_ge(kh_pool, NG + 2)
            pe.wait_ge(kh_dve, NG)
            pe.wait_ge(kh_act, NG + 2)
            pe.wait_ge(bias_set, 2)
            turns(pe, step)

            pe.wait_ge(ld_gate, 2 * 16)
            pe.wait_ge(l_copied, NB)
            for g in range(NG):
                nc.tensor.matmul(bank[g][0:NE, :], gate_w[:], xn2T[:, g * GT:(g + 1) * GT], start=True, stop=True).then_inc(lg_mm, 1)
            pe.wait_ge(lg_copied, NG)
            for b in range(NB):
                last = nc.tensor.transpose(bank[4][:, b * NE:(b + 1) * NE], lgT[:, b * P:(b + 1) * P], ident[0:NE, 0:NE])
            last.then_inc(lg_turned, 1)

            pe.wait_ge(chosen, 1)
            sel = both[:].rearrange("p b e -> p (b e)")
            nc.tensor.matmul(bank[5][:, 0:NB * NE], rows_below[:], sel, start=True, stop=False, skip_group_check=True)
            for n in range(1, NB):
                last = nc.tensor.matmul(bank[5][:, n * NE:NB * NE], ones[:], sel[:, 0:(NB - n) * NE], start=False, stop=(n == NB - 1), skip_group_check=True)
            last.then_inc(ranked, 1)
            for b in range(NB):
                last = nc.tensor.matmul(bank[6][:, 0:NE], ones[:], both[:, b, :], start=(b == 0), stop=(b == NB - 1))
            last.then_inc(ranked, 1)

            pe.wait_ge(table_set, 1)
            pe.wait_ge(ld_w13, 16)
            pe.wait_ge(ld_w2, 16)

            def tile(k, r, i):
                if has(k, 1):
                    t, q = k - 1, (r - 1) % 2
                    e = pe.value_load(expert_of[0:1, bass.ds(t, 1)], min_val=0, max_val=NE - 1)
                    pe.wait_ge(x_copied, t + 1)
                    if not isinstance(t, int) or t >= 2:
                        pe.wait_ge(hid_done, t - 1)
                    nc.tensor.matmul(bank[q][:, 0:HID], xgT[:, q, :], w13[:, bass.ds(e, 1), 0, :].rearrange("p o h -> p (o h)"), start=True, stop=True).then_inc(h1_mm, 1)
                if has(k, 2):
                    t2, q2 = k - 2, r % 2
                    pe.wait_ge(hid_done, t2 + 1)
                    if not isinstance(t2, int) or t2 >= 1:
                        pe.wait_ge(ha_copied, t2)
                        pe.wait_ge(hb_copied, t2)
                    for c in range(2):
                        last = nc.tensor.transpose(bank[4][:, c * P:(c + 1) * P], hid[:, q2, c * P:(c + 1) * P], ident)
                    last.then_inc(ha_turned, 1)
                    c0, cn = CH[2]
                    nc.tensor.transpose(bank[5][0:cn, 0:P], hid[:, q2, c0:c0 + cn], ident).then_inc(hb_turned, 1)
                if has(k, 1):
                    nc.tensor.matmul(bank[2 + q][:, 0:HID], xgT[:, q, :], w13[:, bass.ds(e, 1), 1, :].rearrange("p o h -> p (o h)"), start=True, stop=True).then_inc(h3_mm, 1)
                if has(k, 0):
                    pe.wait_ge(ld_tile[r], i * 16 + 16)
                    if not isinstance(k, int) or k >= 1:
                        pe.wait_ge(x_copied, k)
                    nc.tensor.transpose(bank[6][:, 0:P], xg[:, r, 0:D], ident).then_inc(x_turned, 1)
                if has(k, 2):
                    e2 = pe.value_load(expert_of[0:1, bass.ds(t2, 1)], min_val=0, max_val=NE - 1)
                    pe.wait_ge(ha_copied, t2 + 1)
                    pe.wait_ge(hb_copied, t2 + 1)
                    if not isinstance(t2, int) or t2 >= 1:
                        pe.wait_ge(y_done, t2)
                    for c, (_, cn) in enumerate(CH):
                        last = nc.tensor.matmul(bank[7][:, 0:D], hidT[0:cn, q2, c, :], w2[0:cn, bass.ds(e2, 1), c, :].rearrange("p o d -> p (o d)"),
                                                start=(c == 0), stop=(c == NC - 1))
                    last.then_inc(y_mm, 1)

            tile_turns(pe, tile)


def kernel(x, ctx_2048, mask_BxS2_fk1, g_xattn, g_ffn, L0_xattn_W_src, L0_xattn_b_src, L0_xattn_W_tgt, L0_xattn_b_tgt,
           L0_xattn_W_out, L0_xattn_b_out, L0_ffn_w1, L0_ffn_w2, L0_ffn_w3, L0_ffn_new_w1, L0_ffn_new_w2, L0_ffn_new_w3,
           L0_ffn_gate_weight, L0_ffn_new_gate_weight, L0_ffn_gate_bias):
    import numpy as np
    import concourse.bacc as bacc
    from concourse.bass_utils import run_bass_kernel_spmd

    def split(a):
        return a.reshape(-1, P, a.shape[1]).transpose(1, 0, 2)

    ew1 = np.concatenate([L0_ffn_w1, L0_ffn_new_w1], axis=0)
    ew2 = np.concatenate([L0_ffn_w2, L0_ffn_new_w2], axis=0)
    ew3 = np.concatenate([L0_ffn_w3, L0_ffn_new_w3], axis=0)
    w2_rows = np.zeros((NE, NC * P, D), np.float32)
    w2_rows[:, :HID] = ew2.transpose(0, 2, 1)
    parts = {
        "ident": np.eye(P),
        "head_rows": np.arange(P)[:, None] // HD == np.arange(H),
        "low_first": np.arange(NE, 0, -1),
        "tile_first": np.arange(NB) * P,
        "experts_below": (np.arange(NE)[None, :] < np.arange(NE)[:, None]).reshape(-1),
        "tiles": np.arange(NT),
        "rows_below": np.arange(P)[:, None] < np.arange(P)[None, :],
    }
    consts = np.concatenate([np.broadcast_to(parts[n], (P, w)) for n, w in CONSTS.items()], axis=1).astype(np.float32)
    arrays = {
        "x": x,
        "ctxT": split(np.asarray(ctx_2048).reshape(NB * P, FC * P).T),
        "mask": np.asarray(mask_BxS2_fk1).reshape(-1),
        "maskT": np.asarray(mask_BxS2_fk1).T,
        "g2": np.concatenate([g_xattn, g_ffn]),
        "consts": consts,
        "w_srcT": split(np.asarray(L0_xattn_W_src).T),
        "b_src": L0_xattn_b_src,
        "w_tgtT": np.asarray(L0_xattn_W_tgt).T,
        "b_tgt": L0_xattn_b_tgt,
        "w_outT": split(np.asarray(L0_xattn_W_out).T),
        "b_out": L0_xattn_b_out,
        "w13T": np.stack([ew1.transpose(0, 2, 1), ew3.transpose(0, 2, 1)], axis=2),
        "w2T": w2_rows.reshape(NE, NC, P, D).transpose(0, 2, 1, 3),
        "gateT": np.concatenate([L0_ffn_gate_weight, L0_ffn_new_gate_weight], axis=0).T,
        "gate_b": np.concatenate([np.zeros(NE - 1, np.float32), L0_ffn_gate_bias]),
    }
    arrays = {"in_" + k: np.ascontiguousarray(v) for k, v in arrays.items()}
    nc = bacc.Bacc("TRN2", target_bir_lowering=False, num_devices=1)
    args = [nc.dram_tensor(k, v.shape, mybir.dt.from_np(v.dtype), kind="ExternalInput").ap() for k, v in arrays.items()]
    out = nc.dram_tensor("out_0", (NB, P, D), F32, kind="ExternalOutput").ap()
    x_rows = nc.dram_tensor("x_rows", (NT * P, RW), F32).ap()
    y_rows = nc.dram_tensor("y_rows", (2 * NB * P, D), F32).ap()
    build(nc, *args, x_rows, y_rows, out)
    r = run_bass_kernel_spmd(nc, [arrays], core_ids=[0])
    return r.results[0]["out_0"]
```

```python
from contextlib import ExitStack

import concourse.bass as bass
from concourse import mybir

ALU = mybir.AluOpType
ACT = mybir.ActivationFunctionType
AX = mybir.AxisListType
F32 = mybir.dt.float32
BF16 = mybir.dt.bfloat16
I32 = mybir.dt.int32
F32R = mybir.dt.float32r

P = 128
NB = 16
D = 128
FC = 2
H, HD = 8, 16
HP = 32
UN = 4
NG = NB // UN
GT = UN * P
NE, HID = 9, 352
CH = [(0, 128), (128, 128), (256, 96)]
NC = len(CH)
KH_POOL, KH_DVE = 2, 5
NT = 2 * NB + NE - 1
TR = 8
RW = D + 2
C_ID, C_WEIGHT = D, D + 1
CAP = NB * P + P
PACK, SHIFT = TR // 2, NE
NOWHERE = 1 << 20
SCALE = HD ** -0.5
MASKED = -1.0e30
LN_EPS = 1e-5
TOP_EPS = 1e-20
KNEE = 8.0
FLOOR = -88.72
STRETCH = 1024.0
CONSTS = {"ident": P, "head_rows": H, "experts": NE, "tile_first": NB, "experts_below": NE * NE, "tiles": NT, "rows_below": P,
          "first_rows": NE, "first_ids": 2 * UN, "nowhere": 1, "digits": NT}
NCONST = sum(CONSTS.values())


def build(nc, x, ctxT, mask, maskT, g2, consts, w_srcT, b_src, w_tgtT, b_tgt, w_outT, b_out,
          w13T, w2T, gateT, gate_b, x_rows, y_rows, out):
    with ExitStack() as ctx:
        def sb(name, shape, dt=F32):
            return ctx.enter_context(nc.sbuf_tensor(name, shape, dt))

        def ps(name, shape):
            return ctx.enter_context(nc.psum_tensor(name, shape, F32))

        def sem(name):
            return ctx.enter_context(nc.semaphore(name))

        cst = sb("cst", [P, NCONST])
        at, part = 0, {}
        for name, width in CONSTS.items():
            part[name] = cst[:, at:at + width]
            at += width
        ident, head_rows = part["ident"], part["head_rows"]
        gates, tgates = sb("gates", [P, 2]), sb("tgates", [P, 2])
        w_src = sb("w_src", [P, FC, 2 * D])
        w_tgt = sb("w_tgt", [P, D])
        w_out, w_outg = sb("w_out", [P, 2, D]), sb("w_outg", [P, 2, D])
        b_key, b_qry = sb("b_key", [P, 1]), sb("b_qry", [P, 1])
        b_val = sb("b_val", [P, D])
        b_res, b_resg = sb("b_res", [P, D]), sb("b_resg", [P, D])
        mask_t, live_t = sb("mask_t", [P, NB]), sb("live_t", [P, NB])
        bias_b = sb("bias_b", [P, NB * P], BF16)
        share = sb("share", [P, P], BF16)
        minus_half = sb("minus_half", [P, UN])

        xs = sb("xs", [P, NB, D])
        st1, mv1 = sb("st1", [P, NB, 6]), sb("mv1", [P, NB, 2])
        ve1, rs1 = sb("ve1", [P, NB]), sb("rs1", [P, NB])
        qT = sb("qT", [P, (NB + 1) * P])
        vals = sb("vals", [P, NB, D])

        q_cur = sb("q_cur", [P, UN, P])
        v_cur = sb("v_cur", [P, UN, H, HP])
        mx = sb("mx", [P, 2, H])
        less, probs = sb("less", [P, 2, H]), sb("probs", [P, 2, H, P])
        probsT = sb("probsT", [P, 2, H, P])
        oT = sb("oT", [P, 2, 2, P])
        rden, upd, ulT = sb("rden", [P, 2, H]), sb("upd", [P, 2, D]), sb("ulT", [P, 2, 2, P])
        st2, mv2, ve2, rs2 = sb("st2", [P, 2, 6]), sb("mv2", [P, 2, 2]), sb("ve2", [P, 2]), sb("rs2", [P, 2])
        x2, xn2 = sb("x2", [P, 2, D]), sb("xn2", [P, UN, D])
        xn2_all = sb("xn2_all", [P, NB, D])

        gate_w, gate_bb = sb("gate_w", [P, NE]), sb("gate_bb", [P, NE])
        GZ = UN * NE
        z, logits, sigs = sb("z", [P, GZ]), sb("logits", [P, 2 * GZ + 1]), sb("sigs", [P, 2 * GZ + 1])
        key = sb("key", [P, UN, NE])
        top, top_at, picks = sb("top", [P, UN, 8]), sb("top_at", [P, UN, 8], mybir.dt.uint32), sb("picks", [P, UN, 2])
        choices, chosen_of = sb("choices", [P, 2, UN, NE]), sb("chosen_of", [P, 2, UN, NE])
        slots_of = sb("slots_of", [P, 2, UN, NE])
        both = sb("both", [P, UN, NE], BF16)
        total, sel_sig = sb("total", [P, UN]), sb("sel_sig", [P, 2, UN])
        ranks = sb("ranks", [P, GZ + NE])
        rows_below, ones = sb("rows_below", [P, P], BF16), sb("ones", [P, P], BF16)
        next_row = sb("next_row", [P, NE])
        label, slot_f, slot = sb("label", [P, 2, UN, 2]), sb("slot_f", [P, 2, UN]), sb("slot", [P, 2, UN], I32)
        stage = sb("stage", [P, 2, UN, RW])
        pad_at = sb("pad_at", [1, NE], I32)
        count, filled, below = sb("count", [1, NE]), sb("filled", [1, NE, NB]), sb("below", [1, NE, NE])
        tiles_of, start, end, skip = (sb(n, [1, NE]) for n in ("tiles_of", "start", "end", "skip"))
        skipped, row_f, row_of = sb("skipped", [1, NT, NE]), sb("row_f", [1, NT]), sb("row_of", [1, NT], I32)
        ranked_row = sb("ranked_row", [P, UN, NE])
        passed, expert_f = sb("passed", [1, NT, NE]), sb("expert_f", [1, NT])
        digits, packed_f = sb("digits", [1, NT]), sb("packed_f", [1, NT // PACK])
        experts_packed = sb("experts_packed", [1, NT // PACK + 1], I32)
        pad_row = sb("pad_row", [P, RW])
        ids_in = sb("ids_in", [P, TR], I32)
        xg, xg_high, xg_low, ids, zero = sb("xg", [P, TR, RW]), sb("xg_high", [P, 2, P], F32R), sb("xg_low", [P, 2, P], F32R), sb("ids", [P, TR], I32), sb("zero", [P, 1], I32)
        flat = [t[:].rearrange("p a h t -> p (a h t)") for t in (probs, probsT)]
        gated, hid = (flat[0][:, i * 2 * HID:(i + 1) * 2 * HID].rearrange("p (r h) -> p r h", r=2) for i in range(2))
        hidT = flat[1][:, 0:2 * NC * P].rearrange("p (r c t) -> p r c t", r=2, c=NC)
        yt = flat[1][:, 2 * NC * P:2 * NC * P + TR * D].rearrange("p (r d) -> p r d", r=TR)
        with nc.sbuf_tensor("kheads", [P, H, NB * P], F32) as kheads:
            pass
        w13_high, w13_low = sb("w13_high", [P, NE, 2, HID], F32R), sb("w13_low", [P, NE, 2, HID], F32R)
        w2 = sb("w2", [P, NE, NC, D])
        sb("rest", [P, H * NB * P - NE * (4 * HID + NC * D)])
        with ExitStack() as projections:
            mask_b, ctx_r, xn1, xn1T, kT = (projections.enter_context(nc.sbuf_tensor(n, shape, F32)) for n, shape in (
                ("mask_b", [P, NB * P]), ("ctx_r", [P, 2, FC, GT]), ("xn1", [P, 2, UN, D]), ("xn1T", [P, 2, GT]), ("kT", [P, 2, GT])))
        w13 = sb("w13", [P, NE, 2, HID])
        ys = w13[:].rearrange("p e a h -> p (e a h)")[:, 0:2 * NB * D].rearrange("p (c b d) -> p c b d", c=2, b=NB)

        score_ps = ps("score_ps", [P, 2, H, P])
        pt_ps = ps("pt_ps", [P, 2, UN, P])
        ps_a, ps_b = ps("ps_a", [P, GT]), ps("ps_b", [P, GT])
        bank = [score_ps[:, i // 2, UN * (i % 2):UN * (i % 2) + UN, :] for i in range(4)]
        bank += [pt_ps[:, 0, :, :], pt_ps[:, 1, :, :]]
        bank = [b.rearrange("p a t -> p (a t)") for b in bank] + [ps_a[:, :], ps_b[:, :]]

        ld_first, ld_out, ld_mask, ld_gate = (sem(n) for n in ("ld_first", "ld_out", "ld_mask", "ld_gate"))
        ld_x = [sem(f"ld_x{n}") for n in range(NG)]
        ld_ctx = [sem(f"ld_ctx{n}") for n in range(2)]
        ld_w2, st_pad = sem("ld_w2"), sem("st_pad")
        ld_w13 = [sem(f"ld_w13_{n}") for n in range(NE // 3)]
        st_rows = [sem(f"st_rows{n}") for n in range(UN)]
        ld_tile = [sem(f"ld_tile{n}") for n in range(TR)]
        st_y = [sem(f"st_y{n}") for n in range(TR)]
        ld_y = [[sem(f"ld_y{n}_{c}") for c in range(2)] for n in range(NG)]
        st_out = sem("st_out")
        dve_chain, act_chain, pool_set = sem("dve_chain"), sem("act_chain"), sem("pool_set")
        scaled_w = sem("scaled_w")
        stats1, var1, rstd1, ln1 = sem("stats1"), sem("var1"), sem("rstd1"), sem("ln1")
        xn1_turned, xn1_copied = sem("xn1_turned"), sem("xn1_copied")
        v_mm, k_mm, q_mm, r_mm = sem("v_mm"), sem("k_mm"), sem("q_mm"), sem("r_mm")
        v_done, k_done, q_done, r_done = sem("v_done"), sem("k_done"), sem("q_done"), sem("r_done")
        kh_pool, kh_dve, kh_act, res_done, bias_set = sem("kh_pool"), sem("kh_dve"), sem("kh_act"), sem("res_done"), sem("bias_set")
        q_set, v_set, scores, maxed, lessened, prob = (sem(n) for n in ("q_set", "v_set", "scores", "maxed", "lessened", "prob"))
        pt_a, pt_b, pt_copied, pv, o_copied = sem("pt_a"), sem("pt_b"), sem("pt_copied"), sem("pv"), sem("o_copied")
        o_turned, rdened, normed, ul_turned, ul_copied = (sem(n) for n in ("o_turned", "rdened", "normed", "ul_turned", "ul_copied"))
        o_mm, x2_done, x2_kept, var2, rstd2, ln2 = (sem(n) for n in (
            "o_mm", "x2_done", "x2_kept", "var2", "rstd2", "ln2"))
        lg_mm, lg_kept, lg_ready, sig_exp, route_chain = (sem(n) for n in (
            "lg_mm", "lg_kept", "lg_ready", "sig_exp", "route_chain"))
        ids_copied, kept, w_high, w_low = sem("ids_copied"), sem("kept"), sem("w_high"), sem("w_low")
        pad_set, staged, chosen, ranked, ranks_kept, label_set, pads_known, rows_known, table_set = (sem(n) for n in (
            "pad_set", "staged", "chosen", "ranked", "ranks_kept", "label_set", "pads_known", "rows_known", "table_set"))
        x_turned, x_high, x_low, h1_mm, h3_mm, silu_done, hid_done = (sem(n) for n in (
            "x_turned", "x_high", "x_low", "h1_mm", "h3_mm", "silu_done", "hid_done"))
        ha_turned, hb_turned, ha_copied, hb_copied, y_mm, y_done, y_added = (sem(n) for n in (
            "ha_turned", "hb_turned", "ha_copied", "hb_copied", "y_mm", "y_done", "y_added"))

        block = ctx.enter_context(nc.Block())

        def turns(eng, step):
            for k in range(2 * UN):
                step(k, k % UN, k // UN)
            with eng.Fori(2, NG) as i:
                for r in range(UN):
                    step(i * UN + r, r, i)
            for k in range(NB, NB + 8):
                step(k, k % UN, k // UN)

        def routed(k, i, lag):
            group = i - lag
            return group if not isinstance(k, int) or 0 <= group < NG else None

        def on(k, lag):
            return not isinstance(k, int) or 0 <= k - lag < NB

        def after(b, n):
            return not isinstance(b, int) or b >= n

        def tile_turns(eng, step):
            for k in range(TR):
                step(k, k, 0)
            with eng.Fori(1, NT // TR) as i:
                for r in range(TR):
                    step(i * TR + r, r, i)
            for k in range(NT, NT + 2):
                step(k, k % TR, k // TR)

        def has(k, lag):
            return not isinstance(k, int) or 0 <= k - lag < NT

        @block.sync
        def _(sp):
            sp.dma_start(xs[:, 0:UN, :], x[0:UN].rearrange("b t d -> t b d")).then_inc(ld_x[0], 16)
            sp.dma_start(w_src[:], w_srcT).then_inc(ld_first, 16)
            sp.dma_start(cst[:], consts).then_inc(ld_first, 16)
            sp.dma_start(w_tgt[:], w_tgtT).then_inc(ld_first, 16)
            with sp.Fori(0, NG // 2) as i:
                for r in range(2):
                    sp.wait_ge(r_mm, i * 2 + r + 1)
                    sp.dma_start(ctx_r[:, r, :, :], ctxT[:, :, bass.ds((i * 2 + r) * GT, GT)]).then_inc(ld_ctx[r], 16)
                    sp.dma_start(mask_b[:, bass.ds((i * 2 + r) * GT, GT)], mask[bass.ds((i * 2 + r) * GT, GT)].partition_broadcast(P)).then_inc(ld_ctx[r], 16)
            sp.wait_ge(scores, 2 * UN + 1)
            for n in range(NE // 3):
                sp.dma_start(w13[:, 3 * n:3 * n + 3], w13T[3 * n:3 * n + 3].rearrange("e p a b -> p e a b")).then_inc(ld_w13[n], 16)
            sp.wait_ge(scores, 2 * NB)
            sp.dma_start(w2[:], w2T.rearrange("e p a b -> p e a b")).then_inc(ld_w2, 16)

            sp.wait_ge(pads_known, 1)
            for e in range(0, NE, 2):
                at = sp.value_load(pad_at[0:1, e:e + 1], min_val=e * CAP, max_val=e * CAP + NB * P)
                sp.dma_start(x_rows[bass.ds(at, P), :], pad_row[:]).then_inc(st_pad, 16)
            sp.wait_ge(rows_known, 1)
            rows = [sp.value_load(row_of[0:1, r:r + 1], min_val=0, max_val=NE * CAP) for r in range(TR)]
            sp.wait_ge(st_pad, NE * 16)
            for p in range(UN):
                sp.wait_ge(st_rows[p], NG * 32 + 16)
            for r in range(TR):
                sp.dma_start(xg[:, r, :], x_rows[bass.ds(rows[r], P), :]).then_inc(ld_tile[r], 16)
            with sp.Fori(1, NT // TR) as i:
                for r in range(TR):
                    sp.wait_ge(st_y[r], i * 16)
                    row = sp.value_load(row_of[0:1, bass.ds(i * TR + r, 1)], min_val=0, max_val=NE * CAP)
                    sp.dma_start(xg[:, r, :], x_rows[bass.ds(row, P), :]).then_inc(ld_tile[r], 16)

            for r in range(TR):
                sp.wait_ge(st_y[r], (NT // TR) * 16)
            y_tok = y_rows.rearrange("(c b t) d -> t c b d", c=2, t=P)
            for g in range(NG):
                for c in range(2):
                    sp.dma_start(ys[:, c, g * UN:(g + 1) * UN, :], y_tok[:, c, g * UN:(g + 1) * UN, :]).then_inc(ld_y[g][c], 16)
            for g in range(NG):
                sp.wait_ge(y_added, 2 * g + 2)
                sp.dma_start(out[g * UN:(g + 1) * UN].rearrange("b t d -> t b d"), xs[:, g * UN:(g + 1) * UN, :]).then_inc(st_out, 16)
            sp.wait_ge(st_out, 16 * NG)

        @block.scalar
        def _(act):
            act.dma_start(gates[:], g2.partition_broadcast(P)).then_inc(ld_out, 16)
            act.dma_start(w_out[:], w_outT).then_inc(ld_out, 16)
            act.dma_start(b_res[:], b_out.partition_broadcast(P)).then_inc(ld_out, 16)
            act.dma_start(xs[:, UN:2 * UN, :], x[UN:2 * UN].rearrange("b t d -> t b d")).then_inc(ld_x[1], 16)
            act.dma_start(b_val[:], b_src[D:2 * D].partition_broadcast(P)).then_inc(ld_mask, 16)
            act.dma_start(b_key[:], b_src[0:D].rearrange("(p o) -> p o", o=1)).then_inc(ld_mask, 16)
            act.dma_start(b_qry[:], b_tgt.rearrange("(p o) -> p o", o=1)).then_inc(ld_mask, 16)
            act.dma_start(mask_t[:], maskT).then_inc(ld_mask, 16)
            for n in range(2, NG):
                act.dma_start(xs[:, n * UN:(n + 1) * UN, :], x[n * UN:(n + 1) * UN].rearrange("b t d -> t b d")).then_inc(ld_x[n], 16)
            act.dma_start(gate_w[:], gateT).then_inc(ld_gate, 16)
            act.dma_start(gate_bb[:], gate_b.partition_broadcast(P)).then_inc(ld_gate, 16)

            act.wait_ge(ld_out, 3 * 16)
            nc.scalar.activation(tgates[:], gates[:], ACT.Tanh).then_inc(act_chain, 1)
            act.wait_ge(act_chain, 1)
            nc.scalar.activation(w_outg[:], w_out[:], ACT.Copy, scale=tgates[:, 0:1]).then_inc(scaled_w, 1)
            nc.scalar.activation(b_resg[:], b_res[:], ACT.Copy, scale=tgates[:, 0:1]).then_inc(scaled_w, 1)

            act.wait_ge(ld_first, 3 * 16)
            with act.Fori(0, NG // 2) as i:
                for r in range(2):
                    j = i * 2 + r
                    act.wait_ge(xn1_turned, j + 1)
                    act.wait_ge(r_mm, j + 1)
                    nc.scalar.copy(xn1T[:, r, :], ps_a[:, :]).then_inc(xn1_copied, 1)
                    act.wait_ge(k_done, j + 2)
                    for h in range(KH_DVE, H):
                        last = nc.scalar.activation(kheads[:, h, bass.ds(j * GT, GT)], kT[:, r, :], ACT.Copy,
                                                    scale=head_rows[:, h:h + 1])
                    last.then_inc(kh_act, 1)

            def set_query(b, place):
                if after(b, UN):
                    act.wait_ge(scores, 2 * (b - UN + 1))
                nc.scalar.copy(q_cur[:, place, :], qT[:, bass.ds(b * P, P)]).then_inc(q_set, 1)

            act.wait_ge(q_done, NG + 1)
            set_query(0, 0)

            def exps(k, r, half):
                act.wait_ge(lessened, 2 * k + half + 1)
                if after(k, 2):
                    act.wait_ge(pt_b, k - 1)
                for h in range(half * UN, (half + 1) * UN):
                    last = nc.scalar.activation(probs[:, r % 2, h, :], score_ps[:, r % 2, h, :], ACT.Exp,
                                                bias=less[:, r % 2, h:h + 1], scale=SCALE)
                last.then_inc(prob, 1)

            def step(k, r, i):
                if on(k, 1):
                    b, q = k - 1, (r - 1) % 2
                    if after(b, 2):
                        act.wait_ge(pv, b - 1)
                    act.wait_ge(pt_a, b + 1)
                    nc.scalar.copy(probsT[:, q, 0:UN, :], pt_ps[:, 0, :, :]).then_inc(pt_copied, 1)
                    act.wait_ge(pt_b, b + 1)
                    nc.scalar.copy(probsT[:, q, UN:H, :], pt_ps[:, 1, :, :]).then_inc(pt_copied, 1)
                if on(k, 2) or on(k, 3):
                    act.wait_ge(ul_turned, k - 1)
                    if after(k, 4):
                        act.wait_ge(o_mm, min(k - 3, NB) if isinstance(k, int) else k - 3)
                    low, high = 0 if on(k, 2) else 1, 2 if on(k, 3) else 1
                    nc.scalar.copy(ulT[:, r % 2, low:high, :], ps_b[:, low * P:high * P].rearrange("p (a t) -> p a t", a=high - low)).then_inc(ul_copied, 1)
                if not isinstance(k, int) or k + 1 < NB:
                    set_query(k + 1, (r + 1) % UN)
                if on(k, 0):
                    exps(k, r, 0)
                if on(k, 1):
                    b = k - 1
                    act.wait_ge(pv, b + 1)
                    if after(b, 2):
                        act.wait_ge(o_turned, b - 1)
                    nc.scalar.copy(oT[:, (r - 1) % 2, :, :], ps_a[:, 0:2 * P].rearrange("p (a t) -> p a t", a=2)).then_inc(o_copied, 1)
                if on(k, 0):
                    exps(k, r, 1)
                if r == 2 and routed(k, i, 1) is not None:
                    g = routed(k, i, 1)
                    act.wait_ge(lg_ready, g + 1)
                    if not isinstance(g, int) or g >= 1:
                        act.wait_ge(label_set, g * UN - 2)
                    nc.scalar.activation(sigs[:], logits[:], ACT.Exp, scale=-1.0).then_inc(sig_exp, 1)
                if on(k, 3):
                    b = k - 3
                    act.wait_ge(ln2, b + 1)
                    nc.scalar.copy(xn2_all[:, bass.ds(b, 1), :].rearrange("p o d -> p (o d)"), xn2[:, (r - 3) % UN, :]).then_inc(kept, 1)
                if r in (1, 2) and routed(k, i, 2) is not None:
                    g, p = routed(k, i, 2), (r - 1) * 2
                    act.wait_ge(kept, g * UN + UN)
                    for place in (p, p + 1):
                        act.wait_ge(st_rows[place], g * 32 + 16)
                    nc.scalar.copy(stage[:, :, p:p + 2, 0:D], xn2_all[:, bass.ds(g * UN + p, 2), :].unsqueeze(1).to_broadcast([P, 2, 2, D])).then_inc(staged, 1)

                if isinstance(k, int) and k in (NB + 1, NB + 3, NB + 4):
                    n = (NB + 1, NB + 3, NB + 4).index(k)
                    act.wait_ge(ld_w13[n], 16)
                    act.wait_ge(scores, 2 * NB)
                    for e in range(3 * n, 3 * n + 3):
                        nc.scalar.copy(w13_high[:, e], w13[:, e]).then_inc(w_high, 1)

            turns(act, step)

            act.wait_ge(pads_known, 1)
            for e in range(1, NE, 2):
                at = act.value_load(pad_at[0:1, e:e + 1], min_val=e * CAP, max_val=e * CAP + NB * P)
                act.dma_start(x_rows[bass.ds(at, P), :], pad_row[:]).then_inc(st_pad, 16)

            nc.scalar.preload_act_table(ACT.Silu)
            act.wait_ge(table_set, 1)

            def tile(k, r, i):
                if has(k, 2):
                    t, q = k - 2, r % 2
                    act.wait_ge(ha_turned, t + 1)
                    if not isinstance(t, int) or t >= 2:
                        act.wait_ge(y_mm, t - 1)
                    nc.scalar.copy(hidT[:, q, 0:2, :], bank[4][:, 0:2 * P].rearrange("p (c t) -> p c t", c=2)).then_inc(ha_copied, 1)
                if has(k, 0):
                    act.wait_ge(x_turned, k + 1)
                    if not isinstance(k, int) or k >= 2:
                        act.wait_ge(h3_mm, k - 1)
                    nc.scalar.copy(xg_high[:, r % 2, :], bank[6][:, 0:P]).then_inc(x_high, 1)

                if has(k, 1):
                    t, q = k - 1, (r - 1) % 2
                    act.wait_ge(h1_mm, t + 1)
                    if not isinstance(t, int) or t >= 2:
                        act.wait_ge(hid_done, t - 1)
                    nc.scalar.activation(gated[:, q, :], bank[q][:, 0:HID], ACT.Silu).then_inc(silu_done, 1)
            tile_turns(act, tile)

        @block.gpsimd
        def _(pool):
            nc.gpsimd.memset(minus_half[:], -0.5)
            nc.gpsimd.memset(share[:], 1.0 / P)
            nc.gpsimd.memset(zero[:], 0)
            nc.gpsimd.memset(ones[:], 1.0)
            nc.gpsimd.memset(pad_row[:], 0.0).then_inc(pad_set, 1)
            pool.wait_ge(pad_set, 1)
            nc.gpsimd.memset(v_cur[:], 0.0).then_inc(pool_set, 1)
            pool.wait_ge(pool_set, 1)

            pool.wait_ge(ld_first, 3 * 16)
            nc.gpsimd.tensor_copy(pad_row[:, C_ID:C_ID + 1], part["nowhere"]).then_inc(pad_set, 1)
            for j in range(NG):
                here = slice(j * UN, (j + 1) * UN)
                pool.wait_ge(var1, j + 1)
                nc.gpsimd.tensor_tensor(rs1[:, here], ve1[:, here], minus_half[:], ALU.pow).then_inc(rstd1, 1)
            pool.wait_ge(scaled_w, 2)
            with pool.Fori(0, NG // 2) as i:
                for r in range(2):
                    j = i * 2 + r
                    pool.wait_ge(k_done, j + 2)
                    for h in range(KH_POOL):
                        last = nc.gpsimd.tensor_tensor(kheads[:, h, bass.ds(j * GT, GT)], kT[:, r, :],
                                                       head_rows[:, h:h + 1].to_broadcast([P, GT]), ALU.mult)
                    last.then_inc(kh_pool, 1)
                    pool.wait_ge(r_done, j + 2)
                    here = xs[:, bass.ds(j * UN, UN), :]
                    nc.gpsimd.tensor_tensor(here, here, b_resg[:].unsqueeze(1).to_broadcast([P, UN, D]), ALU.add).then_inc(res_done, 1)

            def step(k, r, i):
                if on(k, 0):
                    if after(k, UN):
                        pool.wait_ge(pv, k - UN + 1)
                    nc.gpsimd.tensor_tensor(v_cur[:, r, :, 0:HD], vals[:, bass.ds(k, 1), :].rearrange("p o (h d) -> p (o h) d", h=H),
                                            mask_t[:, bass.ds(k, 1)].unsqueeze(1).to_broadcast([P, H, HD]), ALU.mult)
                    nc.gpsimd.tensor_copy(v_cur[:, r, :, HD:HD + 1], live_t[:, bass.ds(k, 1)].unsqueeze(1).to_broadcast([P, H, 1])).then_inc(v_set, 1)
                if isinstance(k, int) and UN <= k < 2 * UN:
                    p, n = k - UN, P // UN
                    pool.wait_ge(pad_set, 2)
                    pool.dma_start(x_rows[NE * CAP + p * n:NE * CAP + (p + 1) * n], pad_row[p * n:(p + 1) * n]).then_inc(st_rows[p], 16)
                g = routed(k, i, 2) if r >= 2 else None
                places = {2: (0, 1), 3: (2, 3)}[r] if g is not None else ()
                if places:
                    pool.wait_ge(staged, g * 2 + places[-1] // 2 + 1)
                if places and not isinstance(k, int):
                    pool.wait_ge(label_set, g * UN + places[-1] + 2)
                if on(k, 3):
                    b, q = k - 3, (r - 3) % 2
                    pool.wait_ge(var2, b + 1)
                    nc.gpsimd.tensor_tensor(rs2[:, q:q + 1], ve2[:, q:q + 1], minus_half[:, 0:1], ALU.pow).then_inc(rstd2, 1)
                if places and isinstance(k, int):
                    pool.wait_ge(label_set, g * UN + places[-1] + 2)
                for p in places:
                    for c in range(2):
                        pool.indirect_dma_start(x_rows[:, :], bass.IndirectOffsetOnAxis(ap=slot[:, c, p:p + 1], axis=0), stage[:, c, p, :], None,
                                                bounds_check=last_slot, oob_is_err=False).then_inc(st_rows[p], 16)

            pool.wait_ge(v_done, NG + 1)
            pool.wait_ge(q_done, NG + 1)
            pool.wait_ge(bias_set, 1)
            last_slot = pool.to_reg(NE * CAP - 1)
            turns(pool, step)

            last_row = pool.to_reg(2 * NB * P - 1)

            def tile(k, r, i):
                if has(k, 0):
                    if has(k, 1):
                        pool.wait_ge(ids_copied, k)
                    pool.wait_ge(y_done, k + 1)
                    nc.gpsimd.tensor_tensor(ids[:, r:r + 1], ids_in[:, r:r + 1], zero[:], ALU.add).then_inc(ids_copied, 1)
                if has(k, 1):
                    place = (r - 1) % TR
                    if isinstance(k, int) and k == NT:
                        pool.wait_ge(ids_copied, NT)
                    pool.indirect_dma_start(y_rows[:, :], bass.IndirectOffsetOnAxis(ap=ids[:, place:place + 1], axis=0), yt[:, place, :], None,
                                            bounds_check=last_row, oob_is_err=False).then_inc(st_y[place], 16)

            tile_turns(pool, tile)

        @block.vector
        def _(dve):
            links = [0]

            def link(ins):
                links[0] += 1
                ins.then_inc(dve_chain, 1)
                dve.wait_ge(dve_chain, links[0])

            for s, places in ((v_done, 1), (k_done, 1), (q_done, 1), (r_done, 1), (xn1_copied, 1), (kh_pool, 2), (kh_act, 2),
                              (label_set, 1)):
                dve.sem_inc(s, places)
            nc.vector.memset(qT[:, NB * P:(NB + 1) * P], 0.0)
            nc.vector.memset(logits[:, 2 * GZ:2 * GZ + 1], KNEE).then_inc(r_mm, 2)

            for j in range(NG):
                dve.wait_ge(ld_x[j], 16)
                for b in range(j * UN, (j + 1) * UN):
                    nc.vector.bn_stats(st1[:, b, :], xs[:, b, :]).then_inc(stats1, 1)
                dve.wait_ge(stats1, (j + 1) * UN)
                for b in range(j * UN, (j + 1) * UN):
                    last = nc.vector.bn_aggr(mv1[:, b, :], st1[:, b, :])
                link(last)
                here = slice(j * UN, (j + 1) * UN)
                nc.vector.tensor_scalar(ve1[:, here], mv1[:, here, 1], LN_EPS, None, ALU.add).then_inc(var1, 1)

            dve.wait_ge(ld_mask, 4 * 16)
            dve.wait_ge(ld_first, 3 * 16)
            nc.vector.tensor_scalar(live_t[:], mask_t[:], 0.0, None, ALU.not_equal).then_inc(bias_set, 1)
            nc.vector.tensor_copy(rows_below[:], part["rows_below"])
            nc.vector.tensor_copy(next_row[:], part["first_rows"])
            nc.vector.tensor_copy(label[:, :, :, 0], part["first_ids"].rearrange("p (c b) -> p c b", c=2))
            def norm(j):
                dve.wait_ge(rstd1, j + 1)
                dve.wait_ge(r_mm, j + 1)
                for b in range(UN):
                    at = j * UN + b
                    last = nc.vector.tensor_scalar(xn1[:, j % 2, b, :], xs[:, at, :], mv1[:, at, 0:1], rs1[:, at:at + 1], ALU.subtract, ALU.mult)
                last.then_inc(ln1, 1)

            def spread(j):
                dve.wait_ge(k_done, j + 2)
                for h in range(KH_POOL, KH_DVE):
                    last = nc.vector.tensor_scalar(kheads[:, h, j * GT:(j + 1) * GT], kT[:, j % 2, :], head_rows[:, h:h + 1], None, ALU.mult)
                last.then_inc(kh_dve, 1)

            norm(0)
            for j in range(NG):
                r, here, cols = j % 2, slice(j * UN, (j + 1) * UN), slice(j * GT, (j + 1) * GT)
                dve.wait_ge(v_mm, j + 1)
                nc.vector.tensor_tensor(vals[:, here, :], bank[0].rearrange("p (b d) -> p b d", b=UN),
                                        b_val[:].unsqueeze(1).to_broadcast([P, UN, D]), ALU.add).then_inc(v_done, 1)
                dve.wait_ge(k_mm, j + 1)
                dve.wait_ge(kh_pool, j + 1)
                dve.wait_ge(kh_act, j + 1)
                nc.vector.scalar_tensor_tensor(kT[:, r, :], bank[1], b_key[:, 0:1], mask_b[:, cols], ALU.add, ALU.mult).then_inc(k_done, 1)
                dve.wait_ge(q_mm, j + 1)
                nc.vector.scalar_tensor_tensor(qT[:, cols], bank[2], b_qry[:, 0:1], mask_b[:, cols], ALU.add, ALU.mult).then_inc(q_done, 1)
                nc.vector.tensor_scalar(bias_b[:, cols], mask_b[:, cols], 0.0, MASKED, ALU.is_equal, ALU.mult).then_inc(bias_set, 1)
                if j + 1 == NG:
                    spread(j)
                dve.wait_ge(r_mm, j + 3)
                nc.vector.tensor_tensor(xs[:, here, :], bank[3].rearrange("p (b d) -> p b d", b=UN), xs[:, here, :], ALU.add).then_inc(r_done, 1)
                if j + 1 < NG:
                    norm(j + 1)
                    spread(j)
            route_links = {}
            LINKS = {"clamp": 1, "keys": 4, "choose": 4, "weigh": 5, "place": 3}

            def route_link(g, stage_name, ins):
                route_links[stage_name] = route_links.get(stage_name, 0) + 1
                before = sum(n for name, n in LINKS.items() if list(LINKS).index(name) < list(LINKS).index(stage_name))
                ins.then_inc(route_chain, 1)
                dve.wait_ge(route_chain, g * sum(LINKS.values()) + before + route_links[stage_name])

            high = logits[:, GZ:2 * GZ].rearrange("p (b e) -> p b e", b=UN)
            high_sig = sigs[:, GZ:2 * GZ].rearrange("p (b e) -> p b e", b=UN)

            def clamp(g):
                route_links.clear()
                dve.wait_ge(lg_kept, g * UN + UN)
                nc.vector.tensor_scalar(logits[:, 0:GZ], z[:], FLOOR, None, ALU.max)
                nc.vector.tensor_scalar(logits[:, GZ:2 * GZ], z[:], KNEE, None, ALU.max).then_inc(lg_ready, 1)
                route_link(g, "clamp", nc.vector.tensor_scalar(key[:].rearrange("p b e -> p (b e)"), z[:], FLOOR, KNEE, ALU.max, ALU.min))
                assert route_links["clamp"] == LINKS["clamp"]

            def make_keys(g):
                route_links.clear()
                dve.wait_ge(sig_exp, g + 1)
                route_link(g, "keys", nc.vector.tensor_scalar(sigs[:], sigs[:], 1.0, None, ALU.add))
                route_link(g, "keys", nc.vector.reciprocal(sigs[:], sigs[:]))
                route_link(g, "keys", nc.vector.tensor_scalar(high_sig, high_sig, sigs[:, 2 * GZ:2 * GZ + 1], STRETCH, ALU.subtract, ALU.mult))
                route_link(g, "keys", nc.vector.tensor_tensor(key[:], key[:], high_sig, ALU.add))
                assert route_links["keys"] == LINKS["keys"]

            def choose(g):
                route_links.clear()
                dve.wait_ge(label_set, g * UN + 1)
                nc.vector.tensor_scalar(label[:, 0, :, 0], label[:, 0, :, 0], float(GT), None, ALU.add)
                for b in range(UN):
                    last = nc.vector.max(top[:, b, :], key[:, b, :])
                route_link(g, "choose", last)
                nc.vector.tensor_scalar(label[:, 1, :, 0], label[:, 1, :, 0], float(GT), None, ALU.add)
                for b in range(UN):
                    last = nc.vector.max_index(top_at[:, b, :], top[:, b, :], key[:, b, :])
                route_link(g, "choose", last)
                route_link(g, "choose", nc.vector.tensor_copy(picks[:], top_at[:, :, 0:2]))
                for c in range(2):
                    last = nc.vector.tensor_tensor(choices[:, c, :, :], part["experts"].unsqueeze(1).to_broadcast([P, UN, NE]),
                                                   picks[:, :, c:c + 1].to_broadcast([P, UN, NE]), ALU.is_equal)
                route_link(g, "choose", last)
                assert route_links["choose"] == LINKS["choose"]
                if not isinstance(g, int) or g >= 1:
                    dve.wait_ge(ranked, g)
                nc.vector.tensor_tensor(both[:], choices[:, 0, :, :], choices[:, 1, :, :], ALU.add).then_inc(chosen, 1)

            def of_choices(v):
                return v.unsqueeze(1).to_broadcast([P, 2, GZ])

            flat_choices, flat_of, flat_slots = (t[:].rearrange("p c b e -> p c (b e)") for t in (choices, chosen_of, slots_of))

            def weigh(g):
                route_links.clear()
                dve.wait_ge(chosen, g + 1)
                dve.wait_ge(label_set, g * UN + 1)
                route_link(g, "weigh", nc.vector.tensor_tensor(flat_of, flat_choices, of_choices(sigs[:, 0:GZ]), ALU.mult))
                route_link(g, "weigh", nc.vector.tensor_reduce(sel_sig[:], chosen_of[:], AX.X, ALU.add))
                route_link(g, "weigh", nc.vector.scalar_tensor_tensor(total[:], sel_sig[:, 0, :], TOP_EPS, sel_sig[:, 1, :], ALU.add, ALU.add))
                route_link(g, "weigh", nc.vector.reciprocal(total[:], total[:]))
                route_link(g, "weigh", nc.vector.scalar_tensor_tensor(label[:, :, :, 1], sel_sig[:], tgates[:, 1:2], total[:].unsqueeze(1).to_broadcast([P, 2, UN]),
                                                                      ALU.mult, ALU.mult))
                assert route_links["weigh"] == LINKS["weigh"]

            def place_rows(g):
                route_links.clear()
                dve.wait_ge(ranks_kept, g + 1)
                route_link(g, "place", nc.vector.tensor_tensor(ranked_row[:], ranks[:, 0:GZ].rearrange("p (b e) -> p b e", b=UN),
                                                               next_row[:].unsqueeze(1).to_broadcast([P, UN, NE]), ALU.add))
                nc.vector.tensor_tensor(next_row[:], next_row[:], ranks[:, GZ:GZ + NE], ALU.add)
                route_link(g, "place", nc.vector.tensor_tensor(flat_slots, flat_choices, of_choices(ranked_row[:].rearrange("p b e -> p (b e)")), ALU.mult))
                route_link(g, "place", nc.vector.tensor_reduce(slot_f[:], slots_of[:], AX.X, ALU.add))
                assert route_links["place"] == LINKS["place"]

            def label_places(g, places):
                for p in places:
                    dve.wait_ge(st_rows[p], g * 32 + 16)
                    nc.vector.tensor_copy(stage[:, :, p, C_ID:C_ID + 2], label[:, :, p, :])
                    nc.vector.tensor_copy(slot[:, :, p], slot_f[:, :, p]).then_inc(label_set, 1)

            def maxima(k, r, half):
                here = slice(half * UN, (half + 1) * UN)
                dve.wait_ge(scores, 2 * k + half + 1)
                nc.vector.tensor_reduce(mx[:, r % 2, here], score_ps[:, r % 2, here, :], AX.X, ALU.max).then_inc(maxed, 1)
                dve.wait_ge(maxed, 2 * k + half + 1)
                if after(k, 2):
                    dve.wait_ge(prob, 2 * k - 2)
                nc.vector.tensor_scalar(less[:, r % 2, here], mx[:, r % 2, here], -SCALE, None, ALU.mult).then_inc(lessened, 1)

            def lows(experts):
                dve.wait_ge(scores, 2 * NB)
                for e in experts:
                    dve.wait_ge(w_high, e + 1)
                    nc.vector.tensor_tensor(w13_low[:, e], w13[:, e], w13_high[:, e].bitcast(F32), ALU.subtract).then_inc(w_low, 1)

            def step(k, r, i):
                if on(k, 0):
                    maxima(k, r, 0)
                if on(k, 2):
                    b, q = k - 2, r % 2
                    dve.wait_ge(o_turned, b + 1)
                    turned = ps_b[:, 0:2 * P].rearrange("p (h c) -> p h c", h=H)
                    nc.vector.reciprocal(rden[:, q, :], turned[:, :, HD]).then_inc(rdened, 1)
                    dve.wait_ge(rdened, b + 1)
                    if after(b, 2):
                        dve.wait_ge(ul_turned, k - 3)
                    nc.vector.tensor_tensor(upd[:, q, :].rearrange("p (h d) -> p h d", h=H), turned[:, :, 0:HD],
                                            rden[:, q, :].unsqueeze(2).to_broadcast([P, H, HD]), ALU.mult).then_inc(normed, 1)
                if on(k, 3):
                    b, q = k - 3, (r - 3) % 2
                    dve.wait_ge(rstd2, b + 1)
                    if after(b, UN):
                        dve.wait_ge(kept, b - UN + 1)
                    nc.vector.tensor_scalar(xn2[:, (r - 3) % UN, :], x2[:, q, :], mv2[:, q, 0:1], rs2[:, q:q + 1],
                                            ALU.subtract, ALU.mult).then_inc(ln2, 1)
                if on(k, 0):
                    maxima(k, r, 1)
                if isinstance(k, int) and k == NB + 2:
                    lows(range(0, 1))
                if r == 3 and routed(k, i, 1) is not None:
                    make_keys(routed(k, i, 1))
                if r == 0 and routed(k, i, 2) is not None:
                    choose(routed(k, i, 2))
                if r == 1 and routed(k, i, 2) is not None:
                    weigh(routed(k, i, 2))
                if r == 2 and routed(k, i, 2) is not None:
                    label_places(routed(k, i, 2), (2, 3))
                if on(k, 3):
                    b, place = k - 3, (r - 3) % UN
                    dve.wait_ge(lg_mm, b + 1)
                    if on(k, 2):
                        dve.wait_ge(o_mm, k - 1)
                    nc.vector.tensor_tensor(z[:, place * NE:(place + 1) * NE], ps_b[:, 3 * P:3 * P + NE], gate_bb[:], ALU.add).then_inc(lg_kept, 1)
                if r == 1 and routed(k, i, 2) is not None:
                    g = routed(k, i, 2)
                    dve.wait_ge(ranked, g + 1)
                    nc.vector.tensor_copy(ranks[:], ps_b[:, 3 * P + NE:3 * P + NE + GZ + NE]).then_inc(ranks_kept, 1)
                if on(k, 2):
                    b, q = k - 2, r % 2
                    here = xs[:, bass.ds(b, 1), :].rearrange("p o d -> p (o d)")
                    if isinstance(b, int) and b == 0:
                        dve.wait_ge(res_done, NG)
                    dve.wait_ge(o_mm, b + 1)
                    if after(b, 2):
                        dve.wait_ge(ln2, b - 1)
                    nc.vector.tensor_tensor(x2[:, q, :], ps_b[:, 2 * P:3 * P], here, ALU.add).then_inc(x2_done, 1)
                    dve.wait_ge(x2_done, b * 3 + 1)
                    nc.vector.bn_stats(st2[:, q, :], x2[:, q, :]).then_inc(x2_done, 1)
                    dve.wait_ge(x2_done, b * 3 + 2)
                    nc.vector.tensor_scalar(here, x2[:, q, :], 1.0, None, ALU.mult).then_inc(x2_kept, 1)
                    nc.vector.bn_aggr(mv2[:, q, :], st2[:, q, :]).then_inc(x2_done, 1)
                    dve.wait_ge(x2_done, b * 3 + 3)
                    nc.vector.tensor_scalar(ve2[:, q:q + 1], mv2[:, q, 1:2], LN_EPS, None, ALU.add).then_inc(var2, 1)
                if r == 2 and routed(k, i, 1) is not None:
                    clamp(routed(k, i, 1))
                if r == 1 and routed(k, i, 2) is not None:
                    place_rows(routed(k, i, 2))
                if r == 1 and routed(k, i, 2) is not None:
                    label_places(routed(k, i, 2), (0, 1))

            dve.wait_ge(ld_gate, 2 * 16)
            turns(dve, step)

            nc.vector.tensor_copy(pad_at[:], next_row[0:1]).then_inc(pads_known, 1)
            link(nc.vector.tensor_tensor(count[:], next_row[0:1], part["first_rows"][0:1], ALU.subtract))
            link(nc.vector.tensor_tensor(filled[:], count[:].unsqueeze(2).to_broadcast([1, NE, NB]),
                                         part["tile_first"][0:1].unsqueeze(1).to_broadcast([1, NE, NB]), ALU.is_gt))
            link(nc.vector.tensor_reduce(tiles_of[:], filled[:], AX.X, ALU.add))
            nc.vector.tensor_scalar(skip[:], tiles_of[:], -float(P), float(CAP), ALU.mult, ALU.add)
            link(nc.vector.tensor_tensor(below[:], part["experts_below"][0:1].rearrange("p (e f) -> p e f", e=NE),
                                         tiles_of[:].unsqueeze(1).to_broadcast([1, NE, NE]), ALU.mult))
            link(nc.vector.tensor_reduce(start[:], below[:], AX.X, ALU.add))
            link(nc.vector.tensor_tensor(end[:], start[:], tiles_of[:], ALU.add))
            link(nc.vector.tensor_tensor(passed[:], part["tiles"][0:1].unsqueeze(2).to_broadcast([1, NT, NE]),
                                         end[:].unsqueeze(1).to_broadcast([1, NT, NE]), ALU.is_ge))
            link(nc.vector.tensor_tensor(skipped[:], passed[:], skip[:].unsqueeze(1).to_broadcast([1, NT, NE]), ALU.mult))
            link(nc.vector.tensor_reduce(row_f[:], skipped[:], AX.X, ALU.add))
            link(nc.vector.scalar_tensor_tensor(row_f[:], part["tiles"][0:1], float(P), row_f[:], ALU.mult, ALU.add))
            nc.vector.tensor_scalar(row_of[:], row_f[:], float(NE * CAP), None, ALU.min).then_inc(rows_known, 1)
            link(nc.vector.tensor_reduce(expert_f[:], passed[:], AX.X, ALU.add))
            link(nc.vector.scalar_tensor_tensor(digits[:], expert_f[:], NE - 1.0, part["digits"][0:1], ALU.min, ALU.mult))
            link(nc.vector.tensor_reduce(packed_f[:], digits[:].rearrange("p (n d) -> p n d", d=PACK), AX.X, ALU.add))
            nc.vector.memset(experts_packed[:, NT // PACK:], 0)
            nc.vector.tensor_copy(experts_packed[:, 0:NT // PACK], packed_f[:]).then_inc(table_set, 1)

            lows(range(1, NE))

            def tile(k, r, i):
                if has(k, 2):
                    t, q = k - 2, r % 2
                    dve.wait_ge(hb_turned, t + 1)
                    if not isinstance(t, int) or t >= 2:
                        dve.wait_ge(y_mm, t - 1)
                    n = CH[2][1]
                    nc.vector.tensor_copy(hidT[0:n, q, 2, :], bank[5][0:n, 0:P]).then_inc(hb_copied, 1)
                if has(k, 0):
                    dve.wait_ge(x_high, k + 1)
                    if not isinstance(k, int) or k >= 2:
                        dve.wait_ge(h3_mm, k - 1)
                    nc.vector.tensor_tensor(xg_low[:, r % 2, :], bank[6][:, 0:P], xg_high[:, r % 2, :].bitcast(F32), ALU.subtract).then_inc(x_low, 1)
                if has(k, 1):
                    t, q = k - 1, (r - 1) % 2
                    dve.wait_ge(silu_done, t + 1)
                    dve.wait_ge(h3_mm, t + 1)
                    if not isinstance(t, int) or t >= 2:
                        dve.wait_ge(hb_turned, t - 1)
                    nc.vector.tensor_tensor(hid[:, q, :], gated[:, q, :], bank[2 + q][:, 0:HID], ALU.mult).then_inc(hid_done, 1)
                if has(k, 2):
                    t, place = k - 2, (r - 2) % TR
                    turn = i if r >= 2 else i - 1
                    dve.wait_ge(y_mm, t + 1)
                    if not isinstance(k, int) or t >= TR:
                        dve.wait_ge(st_y[place], turn * 16)
                    nc.vector.tensor_copy(ids_in[:, place:place + 1], xg[:, place, C_ID:C_ID + 1])
                    nc.vector.tensor_scalar(yt[:, place, :], bank[7][:, 0:D], xg[:, place, C_WEIGHT:C_WEIGHT + 1], None, ALU.mult).then_inc(y_done, 1)

            tile_turns(dve, tile)

            for g in range(NG):
                here = slice(g * UN, (g + 1) * UN)
                for c in range(2):
                    dve.wait_ge(ld_y[g][c], 16)
                    nc.vector.tensor_tensor(xs[:, here, :], xs[:, here, :], ys[:, c, here, :], ALU.add).then_inc(y_added, 1)
                    dve.wait_ge(y_added, 2 * g + c + 1)

        @block.tensor
        def _(pe):
            pe.wait_ge(ld_first, 3 * 16)
            with pe.Fori(0, NG // 2) as i:
                for r in range(2):
                    j = i * 2 + r
                    pe.wait_ge(ld_ctx[r], i * 32 + 32)
                    pe.wait_ge(v_done, j + 1)
                    for b in range(UN):
                        for f in range(FC):
                            last = nc.tensor.matmul(bank[0][:, b * P:(b + 1) * P], ctx_r[:, r, f, b * P:(b + 1) * P], w_src[:, f, D:2 * D],
                                                    start=(f == 0), stop=(f == FC - 1))
                    last.then_inc(v_mm, 1)
                    pe.wait_ge(ln1, j + 1)
                    pe.wait_ge(xn1_copied, j + 1)
                    for b in range(UN):
                        last = nc.tensor.transpose(ps_a[:, b * P:(b + 1) * P], xn1[:, r, b, :], ident)
                    last.then_inc(xn1_turned, 1)
                    pe.wait_ge(k_done, j + 1)
                    for f in range(FC):
                        last = nc.tensor.matmul(bank[1], w_src[:, f, 0:D], ctx_r[:, r, f, :], start=(f == 0), stop=(f == FC - 1))
                    last.then_inc(k_mm, 1)
                    pe.wait_ge(xn1_copied, j + 2)
                    pe.wait_ge(q_done, j + 1)
                    nc.tensor.matmul(bank[2], w_tgt[:], xn1T[:, r, :], start=True, stop=True).then_inc(q_mm, 1)
                    pe.wait_ge(scaled_w, 2)
                    pe.wait_ge(r_done, j + 1)
                    for b in range(UN):
                        last = nc.tensor.matmul(bank[3][:, b * P:(b + 1) * P], xn1T[:, r, b * P:(b + 1) * P], w_outg[:, 0, :], start=True, stop=True)
                    last.then_inc(r_mm, 1)

            def score_half(k, r, half, part_of):
                dst = score_ps[:, r % 2, half * UN:(half + 1) * UN, :]
                if part_of == "products":
                    nc.tensor.matmul(dst, q_cur[:, r, :], kheads[:, half * UN:(half + 1) * UN, bass.ds(k * P, P)], start=True, stop=False)
                else:
                    nc.tensor.matmul(dst, share[:], bias_b[:, bass.ds(k * P, P)].unsqueeze(1).to_broadcast([P, UN, P]),
                                     start=False, stop=True).then_inc(scores, 1)

            def step(k, r, i):
                if isinstance(k, int) and k == 1:
                    pe.wait_ge(q_done, NG + 1)
                    pe.wait_ge(r_done, NG + 1)
                if isinstance(k, int) and k == UN:
                    pe.wait_ge(kh_pool, NG + 2)
                    pe.wait_ge(kh_dve, NG)
                    pe.wait_ge(kh_act, NG + 2)
                    pe.wait_ge(bias_set, 1 + NG)
                if on(k, 0):
                    pe.wait_ge(q_set, k + 1)
                    if after(k, 2):
                        pe.wait_ge(prob, 2 * k - 2)
                    score_half(k, r, 0, "products")
                    score_half(k, r, 0, "bias")
                if on(k, 2):
                    b, q = k - 2, r % 2
                    pe.wait_ge(o_copied, b + 1)
                    if after(b, 1):
                        pe.wait_ge(x2_done, (b - 1) * 3 + 1)
                    for a in range(2):
                        last = nc.tensor.transpose(ps_b[:, a * P:(a + 1) * P], oT[:, q, a, :], ident)
                    last.then_inc(o_turned, 1)
                if on(k, 1):
                    b, q = k - 1, (r - 1) % 2
                    for half, done in enumerate((pt_a, pt_b)):
                        pe.wait_ge(prob, 2 * b + half + 1)
                        if after(b, 1):
                            pe.wait_ge(pt_copied, b * 2 - 1 + half)
                        for h in range(UN):
                            last = nc.tensor.transpose(pt_ps[:, half, h, :], probs[:, q, half * UN + h, :], ident)
                        last.then_inc(done, 1)
                if on(k, 0):
                    score_half(k, r, 1, "products")
                    score_half(k, r, 1, "bias")
                if on(k, 2):
                    pe.wait_ge(normed, k - 1)
                    last = nc.tensor.transpose(ps_b[:, 0:P], upd[:, r % 2, :], ident)
                if on(k, 3):
                    pe.wait_ge(ln2, k - 2)
                    if not on(k, 2):
                        pe.wait_ge(x2_done, NB * 3 - 2)
                    last = nc.tensor.transpose(ps_b[:, P:2 * P], xn2[:, (r - 3) % UN, :], ident)
                if on(k, 2) or on(k, 3):
                    last.then_inc(ul_turned, 1)
                if on(k, 1):
                    b, q, place = k - 1, (r - 1) % 2, (r - 1) % UN
                    pe.wait_ge(v_set, b + 1)
                    if after(b, 1):
                        pe.wait_ge(o_copied, b)
                    for h in range(H):
                        pe.wait_ge(pt_copied, b * 2 + 1 + h // UN) if h % UN == 0 else None
                        row = HP * (h % UN)
                        last = nc.tensor.matmul(ps_a[row:row + HP, (h // UN) * P:(h // UN + 1) * P], v_cur[:, place, h, :], probsT[:, q, h, :],
                                                start=True, stop=True, tile_position=(0, row))
                    last.then_inc(pv, 1)
                if on(k, 2) or on(k, 3):
                    pe.wait_ge(ul_copied, k - 1)
                if on(k, 3):
                    nc.tensor.matmul(ps_b[:, 3 * P:3 * P + NE], ulT[:, r % 2, 1, :], gate_w[:], start=True, stop=True).then_inc(lg_mm, 1)
                if r == 1 and routed(k, i, 2) is not None:
                    pe.wait_ge(chosen, routed(k, i, 2) + 1)
                    sel, at = both[:].rearrange("p b e -> p (b e)"), 3 * P + NE
                    nc.tensor.matmul(ps_b[:, at:at + GZ], rows_below[:], sel, start=True, stop=False, skip_group_check=True)
                    for n in range(1, UN):
                        nc.tensor.matmul(ps_b[:, at + n * NE:at + GZ], ones[:], sel[:, 0:(UN - n) * NE], start=False, stop=(n == UN - 1), skip_group_check=True)
                    for b in range(UN):
                        last = nc.tensor.matmul(ps_b[:, at + GZ:at + GZ + NE], ones[:], both[:, b, :], start=(b == 0), stop=(b == UN - 1), skip_group_check=True)
                    last.then_inc(ranked, 1)
                if on(k, 2):
                    b, q = k - 2, r % 2
                    nc.tensor.matmul(ps_b[:, 2 * P:3 * P], ulT[:, q, 0, :], w_outg[:, 1, :], start=True, stop=True).then_inc(o_mm, 1)

            pe.wait_ge(v_done, NG + 1)
            pe.wait_ge(k_done, NG + 1)
            pe.wait_ge(kh_pool, 2 + 2)
            pe.wait_ge(kh_dve, 2)
            pe.wait_ge(kh_act, 2 + 2)
            pe.wait_ge(bias_set, 1 + 2)
            pe.wait_ge(ld_gate, 2 * 16)
            turns(pe, step)

            pe.wait_ge(table_set, 1)
            pe.wait_ge(w_low, NE)
            pe.wait_ge(ld_w2, 16)

            early, late, unpacked = pe.alloc_register("early"), pe.alloc_register("late"), {}

            def unpack_next(i, n):
                pe.reg_load(late if n % 2 else early, experts_packed[0:1, bass.ds(i * 2 + n, 1)])

            def expert(at):
                if at not in unpacked:
                    pack = pe.snap(early if 0 <= at < PACK else late, min_val=0, max_val=SHIFT ** PACK - 1)
                    unpacked[at] = pe.snap(pack // SHIFT ** (at % PACK) % SHIFT)
                return unpacked[at]

            def hidden(dst, q, e, a):
                def of(w):
                    return w[:, bass.ds(e, 1), a, :].rearrange("p o h -> p (o h)")

                nc.tensor.matmul(dst[:, 0:HID], xg_low[:, q, :], of(w13_high), start=True, stop=False)
                nc.tensor.matmul(dst[:, 0:HID], xg_high[:, q, :], of(w13_low), start=False, stop=False)
                return nc.tensor.matmul(dst[:, 0:HID], xg_high[:, q, :], of(w13_high), start=False, stop=True)

            unpack_next(0, 0)

            def tile(k, r, i):
                if r == 0:
                    unpacked.clear()
                if has(k, 0):
                    if r % PACK == PACK - 1:
                        unpack_next(i, r // PACK + 1)
                    pe.wait_ge(ld_tile[r], i * 16 + 16)
                    if not isinstance(k, int) or k >= 1:
                        pe.wait_ge(x_low, k)
                    nc.tensor.transpose(bank[6][:, 0:P], xg[:, r, 0:D], ident).then_inc(x_turned, 1)
                if has(k, 2):
                    t2, q2 = k - 2, r % 2
                    e2 = expert(r - 2)
                    pe.wait_ge(hid_done, t2 + 1)
                    if not isinstance(t2, int) or t2 >= 1:
                        pe.wait_ge(ha_copied, t2)
                        pe.wait_ge(hb_copied, t2)
                    for c in range(2):
                        last = nc.tensor.transpose(bank[4][:, c * P:(c + 1) * P], hid[:, q2, c * P:(c + 1) * P], ident)
                    last.then_inc(ha_turned, 1)
                    c0, cn = CH[2]
                    nc.tensor.transpose(bank[5][0:cn, 0:P], hid[:, q2, c0:c0 + cn], ident).then_inc(hb_turned, 1)
                if has(k, 1):
                    t, q = k - 1, (r - 1) % 2
                    e = expert(r - 1)
                    pe.wait_ge(x_low, t + 1)
                    if not isinstance(t, int) or t >= 2:
                        pe.wait_ge(hid_done, t - 1)
                    hidden(bank[q], q, e, 0).then_inc(h1_mm, 1)
                    hidden(bank[2 + q], q, e, 1).then_inc(h3_mm, 1)
                if has(k, 2):
                    pe.wait_ge(ha_copied, t2 + 1)
                    pe.wait_ge(hb_copied, t2 + 1)
                    if not isinstance(t2, int) or t2 >= 1:
                        pe.wait_ge(y_done, t2)
                    for c, (_, cn) in enumerate(CH):
                        last = nc.tensor.matmul(bank[7][:, 0:D], hidT[0:cn, q2, c, :], w2[0:cn, bass.ds(e2, 1), c, :].rearrange("p o d -> p (o d)"),
                                                start=(c == 0), stop=(c == NC - 1))
                    last.then_inc(y_mm, 1)

            tile_turns(pe, tile)


def kernel(x, ctx_2048, mask_BxS2_fk1, g_xattn, g_ffn, L0_xattn_W_src, L0_xattn_b_src, L0_xattn_W_tgt, L0_xattn_b_tgt,
           L0_xattn_W_out, L0_xattn_b_out, L0_ffn_w1, L0_ffn_w2, L0_ffn_w3, L0_ffn_new_w1, L0_ffn_new_w2, L0_ffn_new_w3,
           L0_ffn_gate_weight, L0_ffn_new_gate_weight, L0_ffn_gate_bias):
    import numpy as np
    import concourse.bacc as bacc
    from concourse.bass_utils import run_bass_kernel_spmd

    def split(a):
        return a.reshape(-1, P, a.shape[1]).transpose(1, 0, 2)

    ew1 = np.concatenate([L0_ffn_w1, L0_ffn_new_w1], axis=0)
    ew2 = np.concatenate([L0_ffn_w2, L0_ffn_new_w2], axis=0)
    ew3 = np.concatenate([L0_ffn_w3, L0_ffn_new_w3], axis=0)
    w2_rows = np.zeros((NE, NC * P, D), np.float32)
    w2_rows[:, :HID] = ew2.transpose(0, 2, 1)
    parts = {
        "ident": np.eye(P),
        "head_rows": np.arange(P)[:, None] // HD == np.arange(H),
        "experts": np.arange(NE),
        "tile_first": np.arange(NB) * P,
        "experts_below": (np.arange(NE)[None, :] < np.arange(NE)[:, None]).reshape(-1),
        "tiles": np.arange(NT),
        "first_rows": np.arange(NE) * CAP,
        "first_ids": (np.arange(2)[:, None] * NB * P + np.arange(UN) * P).reshape(1, -1) + np.arange(P)[:, None] - GT,
        "nowhere": NOWHERE + np.arange(P)[:, None],
        "digits": np.tile(float(SHIFT) ** np.arange(PACK), NT // PACK),
        "rows_below": np.arange(P)[:, None] < np.arange(P)[None, :],
    }
    consts = np.concatenate([np.broadcast_to(parts[n], (P, w)) for n, w in CONSTS.items()], axis=1).astype(np.float32)
    arrays = {
        "x": x,
        "ctxT": split(np.asarray(ctx_2048).reshape(NB * P, FC * P).T),
        "mask": np.asarray(mask_BxS2_fk1).reshape(-1),
        "maskT": np.asarray(mask_BxS2_fk1).T,
        "g2": np.concatenate([g_xattn, g_ffn]),
        "consts": consts,
        "w_srcT": split(np.asarray(L0_xattn_W_src).T),
        "b_src": L0_xattn_b_src,
        "w_tgtT": np.asarray(L0_xattn_W_tgt).T,
        "b_tgt": L0_xattn_b_tgt,
        "w_outT": split(np.asarray(L0_xattn_W_out).T),
        "b_out": L0_xattn_b_out,
        "w13T": np.stack([ew1.transpose(0, 2, 1), ew3.transpose(0, 2, 1)], axis=2),
        "w2T": w2_rows.reshape(NE, NC, P, D).transpose(0, 2, 1, 3),
        "gateT": np.concatenate([L0_ffn_gate_weight, L0_ffn_new_gate_weight], axis=0).T,
        "gate_b": np.concatenate([np.zeros(NE - 1, np.float32), L0_ffn_gate_bias]),
    }
    arrays = {"in_" + k: np.ascontiguousarray(v) for k, v in arrays.items()}
    nc = bacc.Bacc("TRN2", target_bir_lowering=False, num_devices=1)
    args = [nc.dram_tensor(k, v.shape, mybir.dt.from_np(v.dtype), kind="ExternalInput").ap() for k, v in arrays.items()]
    out = nc.dram_tensor("out_0", (NB, P, D), F32, kind="ExternalOutput").ap()
    x_rows = nc.dram_tensor("x_rows", (NE * CAP + P, RW), F32).ap()
    y_rows = nc.dram_tensor("y_rows", (2 * NB * P, D), F32).ap()
    build(nc, *args, x_rows, y_rows, out)
    r = run_bass_kernel_spmd(nc, [arrays], core_ids=[0])
    return r.results[0]["out_0"]
```
